# Optimizing a Trainium2 kernel written in Bass

```python
import numpy as np
import jax
import jax.numpy as jnp

def _softmax(x, axis=-1):
    return jax.nn.softmax(x, axis=axis)

def _gelu(x):
    return jax.nn.gelu(x, approximate=True)

def _silu(x):
    return jax.nn.silu(x)

def _sigmoid(x):
    return jax.nn.sigmoid(x)

def _layernorm(x, axis=-1, eps=1e-05):
    m = jnp.mean(x, axis=axis, keepdims=True)
    v = jnp.var(x, axis=axis, keepdims=True)
    return (x - m) / jnp.sqrt(v + eps)

def _scatter_add(tgt, idx, src, axis=0):
    return tgt.at[idx].add(src)

def _segment_sum(src, seg, n):
    return jax.ops.segment_sum(src, seg, n)
kernel_name = 'mk_sandwich_d1_jaxref_r8_15763e'

def setup_inputs(seed: int=0):
    np.random.seed(seed)
    _w = jnp.asarray

    def _L0_attn_setup():
        import jax, jax.numpy as jnp
        import numpy as np
        import math
        B, S, D = (4, 256, 128)
        H = 16
        HD = D // H
        DL = 32
        LAMBDA_DECAY = 0.01
        key = jax.random.key(seed)
        ks = jax.random.split(key, 8)
        sc = lambda fan_in: 1.0 / math.sqrt(fan_in)
        return {'x': jax.random.normal(ks[0], (B, S, D), dtype=jnp.float32), 'W_q': jax.random.normal(ks[1], (D, D), dtype=jnp.float32) * sc(D), 'W_k': jax.random.normal(ks[2], (D, D), dtype=jnp.float32) * sc(D), 'W_v': jax.random.normal(ks[3], (D, D), dtype=jnp.float32) * sc(D), 'W_o': jax.random.normal(ks[4], (D, D), dtype=jnp.float32) * sc(D), 'W_down_kv': jax.random.normal(ks[5], (D, DL), dtype=jnp.float32) * sc(D), 'W_up_k': jax.random.normal(ks[6], (DL, D), dtype=jnp.float32) * sc(DL), 'W_up_v': jax.random.normal(ks[7], (DL, D), dtype=jnp.float32) * sc(DL)}
    _L0_attn_in = _L0_attn_setup()

    def _L0_ffn_setup():
        import jax, jax.numpy as jnp
        import numpy as np
        DIM = 128
        HIDDEN = 384
        SCALE = 1.0 / 127.0

        def _dequant(w_int, dtype):
            return w_int.astype(dtype) * jnp.asarray(SCALE, dtype)
        key = jax.random.key(seed)
        k_x, k_g, k_u, k_d = jax.random.split(key, 4)
        x = jax.random.normal(k_x, (4, 256, DIM), dtype=jnp.float32)
        w_gate = jax.random.randint(k_g, (HIDDEN, DIM), -127, 128, dtype=jnp.int32)
        w_up = jax.random.randint(k_u, (HIDDEN, DIM), -127, 128, dtype=jnp.int32)
        w_down = jax.random.randint(k_d, (DIM, HIDDEN), -127, 128, dtype=jnp.int32)
        return {'x': x, 'w_gate': w_gate, 'w_up': w_up, 'w_down': w_down}
    _L0_ffn_in = _L0_ffn_setup()
    _d = {'L0_attn_x': _L0_attn_in['x'], 'L0_attn_W_q': _L0_attn_in['W_q'], 'L0_attn_W_k': _L0_attn_in['W_k'], 'L0_attn_W_v': _L0_attn_in['W_v'], 'L0_attn_W_o': _L0_attn_in['W_o'], 'L0_attn_W_down_kv': _L0_attn_in['W_down_kv'], 'L0_attn_W_up_k': _L0_attn_in['W_up_k'], 'L0_attn_W_up_v': _L0_attn_in['W_up_v'], 'L0_ffn_w_gate': _L0_ffn_in['w_gate'], 'L0_ffn_w_up': _L0_ffn_in['w_up'], 'L0_ffn_w_down': _L0_ffn_in['w_down']}
    _x0 = _d['L0_attn_x']
    _d['L0_attn_x'] = jax.random.normal(jax.random.fold_in(jax.random.key(seed), 1), (8, 512, 128), dtype=_x0.dtype)
    del _x0
    return _d

def reference(L0_attn_x, L0_attn_W_q, L0_attn_W_k, L0_attn_W_v, L0_attn_W_o, L0_attn_W_down_kv, L0_attn_W_up_k, L0_attn_W_up_v, L0_ffn_w_gate, L0_ffn_w_up, L0_ffn_w_down):

    def _L0_attn_ref(x, W_q, W_k, W_v, W_o, W_down_kv, W_up_k, W_up_v):
        import jax, jax.numpy as jnp
        import numpy as np
        import math
        B, S, D = (4, 256, 128)
        H = 16
        HD = D // H
        DL = 32
        LAMBDA_DECAY = 0.01
        b, s, d = x.shape
        q = x @ W_q
        k = x @ W_k
        v = x @ W_v
        latent_kv = (k + v) @ W_down_kv
        k_rec = (latent_kv @ W_up_k).reshape(b, s, H, HD).transpose(0, 2, 1, 3)
        v_rec = (latent_kv @ W_up_v).reshape(b, s, H, HD).transpose(0, 2, 1, 3)
        qh = q.reshape(b, s, H, HD).transpose(0, 2, 1, 3)
        scores = jnp.einsum('bhqd,bhkd->bhqk', qh, k_rec) / math.sqrt(d)
        t = jnp.arange(s, dtype=jnp.float32)
        decay = jnp.exp(-LAMBDA_DECAY * jnp.abs(t[:, None] - t[None, :]))
        scores = scores * decay[None, None, :, :]
        attn = jax.nn.softmax(scores, axis=-1)
        out = jnp.einsum('bhqk,bhkd->bhqd', attn, v_rec)
        out = out.transpose(0, 2, 1, 3).reshape(b, s, d)
        return out @ W_o

    def _L0_ffn_ref(x, w_gate, w_up, w_down):
        import jax, jax.numpy as jnp
        import numpy as np
        DIM = 128
        HIDDEN = 384
        SCALE = 1.0 / 127.0

        def _dequant(w_int, dtype):
            return w_int.astype(dtype) * jnp.asarray(SCALE, dtype)
        wg = _dequant(w_gate, x.dtype)
        wu = _dequant(w_up, x.dtype)
        wd = _dequant(w_down, x.dtype)
        gate = jnp.einsum('bsd,hd->bsh', x, wg)
        up = jnp.einsum('bsd,hd->bsh', x, wu)
        h = jax.nn.silu(gate) * up
        return jnp.einsum('bsh,dh->bsd', h, wd)
    x = L0_attn_x
    x = x + _layernorm(_L0_attn_ref(_layernorm(x, axis=-1), L0_attn_W_q, L0_attn_W_k, L0_attn_W_v, L0_attn_W_o, L0_attn_W_down_kv, L0_attn_W_up_k, L0_attn_W_up_v), axis=-1)
    x = x + _layernorm(_L0_ffn_ref(_layernorm(x, axis=-1), L0_ffn_w_gate, L0_ffn_w_up, L0_ffn_w_down), axis=-1)
    return x

_drawn_inputs = setup_inputs


def setup_inputs(seed=0):
    import zlib

    import numpy as np

    out = dict(_drawn_inputs(seed))
    spreads = {}
    factors = {}
    for name, (base, spread) in spreads.items():
        noise = np.random.default_rng([zlib.crc32(name.encode()), seed]).standard_normal(out[name].shape)
        drawn = base * np.exp(spread * noise) if base else spread * noise
        out[name] = jnp.asarray(drawn.astype(out[name].dtype))
    for name, factor in factors.items():
        out[name] = (out[name] * factor).astype(out[name].dtype)
    return out
```

```python
from contextlib import ExitStack

import concourse.bass as bass
from concourse import mybir

F32 = mybir.dt.float32
BF16 = mybir.dt.bfloat16
I32 = mybir.dt.int32
ALU = mybir.AluOpType
ACT = mybir.ActivationFunctionType

B, S, D = 8, 512, 128
H, HD, DL = 16, 8, 32
HID = 384
P = 128
T = S // P
J = HID // P
HG = 4
NG = H // HG
SLOTS = 2 * T * NG
GS = SLOTS // NG
DECAY = 0.01
SCORE_SCALE = 1.0 / float(D) ** 0.5
DEQUANT = 1.0 / 127.0
EPS = 1e-5
Q_PART = (0, 0, 0, 1, 1, 2)
K_PART = (0, 1, 2, 0, 1, 0)
ROWS = HD * len(Q_PART)
MAX_ROW = 2 * ROWS
ALL_ROWS = MAX_ROW + 3
QA, QB, KA, KB = range(4)

PRE = {1: ("xT", 0), 2: ("q", 0), 5: ("k", 0), 7: ("v", 0), 30: ("maxT", 0)}
ATT = {6: ("maxT", 1), 14: ("maxT", 2), 22: ("maxT", 3), 11: ("oT", 0), 19: ("oT", 1), 27: ("oT", 2)}
POST = {3: ("oT", 3), 4: ("aT", 0), 8: ("y", 0), 10: ("x1T", 0), 12: ("gate", 0), 13: ("up", 0),
        15: ("gate", 1), 16: ("up", 1), 17: ("gate", 2), 18: ("up", 2), 21: ("down", 0)}
MAX_TILES = (3, 3, 3, 3, 2, 2, 0, 0)


def started(n):
    return max(n, 0) if isinstance(n, int) else n


def runs(p):
    if not isinstance(p, int):
        return True, True, True
    return p + 1 < B, 0 <= p < B, p >= 1


def jobs(p):
    pre, att, post = runs(p)
    return {**(PRE if pre else {}), **(ATT if att else {}), **(POST if post else {})}


def job_number(p, slot):
    def whole(n):
        return min(n, B) if isinstance(n, int) else n
    before = len(PRE) * whole(p + 1) + len(ATT) * started(p) + len(POST) * started(p - 1)
    return before + sum(s <= slot for s in jobs(p))


def max_group(p, slot):
    return p * NG + slot // GS + 1


def has_max(p, slot):
    pre, att, _ = runs(p)
    return pre if slot // GS == NG - 1 else att


def wait(eng, sem, n):
    if isinstance(n, int) and n <= 0:
        return
    eng.wait_ge(sem, n)


def sandwich(nc, x, w_q, w_k, w_v, w_o, w_dkv, w_uk, w_uv, w_gate, w_up, w_down, out):
    with ExitStack() as ctx:
        def sb(name, shape, dt=F32):
            return ctx.enter_context(nc.sbuf_tensor(name, shape, dt))

        def psum(name, shape):
            return ctx.enter_context(nc.psum_tensor(name, shape, F32))

        def sem(name):
            return ctx.enter_context(nc.semaphore(name))

        spill = nc.dram_tensor("qk_parts", (P, 3, 4, S), BF16, kind="Internal").ap()

        score = psum("score", [P, 2, 2, S])
        rowscore = psum("rowscore", [P, 2, S])
        o_acc = psum("o_acc", [P, S])
        work = psum("work", [P, S])

        q_op = [sb(f"q_op{i}", [P, H, S], BF16) for i in range(2)]
        ka_op = [sb(f"ka_op{i}", [P, H, S], BF16) for i in range(2)]
        kb_op = [sb(f"kb_op{i}", [P, H, S], BF16) for i in range(2)]
        v_op = [sb(f"v_op{i}", [P, T, H, 32]) for i in range(2)]
        probs = sb("probs", [P, 4, 2, S])
        forms = sb("forms", [P, 4, S])
        parts = sb("parts", [P, 3, 4, S], BF16)
        qk = sb("qk", [P, 2, S])
        x_in = sb("x_in", [P, T, D])
        x_res = sb("x_res", [P, T, D])
        xn = sb("xn", [P, T, D])
        xn_t = sb("xn_t", [P, S])
        o_sb = sb("o_sb", [P, S])
        attn = sb("attn", [P, T, D])
        yn = sb("yn", [P, T, D])
        x1 = sb("x1", [P, T, D])
        x1n, x1n_t = attn, xn_t
        th = sb("th", [P, S])
        attn_t = th
        hid = sb("hid", [P, J, S])
        row_max = sb("row_max", [P, HG * T])
        max_junk = sb("max_junk", [P, 2, S], BF16)
        neg_max = sb("neg_max", [HG * T, 3, P], BF16)
        max_rest = sb("max_rest", [HG * T, P])
        den = sb("den", [P, T, HG])
        stats = [sb(f"stats{i}", [P, T, 6]) for i in range(4)]
        moments = [sb(f"moments{i}", [P, T, 2]) for i in range(4)]
        rstd = [sb(f"rstd{i}", [P, T]) for i in range(4)]

        ident = sb("ident", [P, P])
        minus_half = sb("minus_half", [P, T])
        grow = sb("grow", [P, 3, S])
        fix_row = sb("fix_row", [P, S + (T - 1) * P])
        fix_key = sb("fix_key", [P, P])
        wq_sb = sb("wq_sb", [P, D])
        wo_sb = sb("wo_sb", [P, D])
        wkv = sb("wkv", [P, 2, D])
        wd_sb = sb("wd_sb", [P, DL])
        wup = sb("wup", [DL, 2, D])
        wkv_sum_t = sb("wkv_sum_t", [P, D])
        lat_t = sb("lat_t", [DL, D])
        wkv_full = sb("wkv_full", [P, 2, D])
        w_int = xn[:, 0:J, :].bitcast(I32), x1n[:, 0:J, :].bitcast(I32), yn[:, 0:J, :].bitcast(I32)
        w_raw = forms[:, 0:3, 0:HID]
        wffn = sb("wffn", [P, 3, J, P])

        x_tiles = x.rearrange("b (t p) d -> b p t d", p=P)
        out_tiles = out.rearrange("b (t p) d -> b p t d", p=P)

        x_loaded, xres_loaded, stored = sem("x_loaded"), sem("xres_loaded"), sem("stored")
        w_loaded, spilled, operands_in, max_in = sem("w_loaded"), sem("spilled"), sem("operands_in"), sem("max_in")
        const_ready, exp_ready, grow_ready = sem("const_ready"), sem("exp_ready"), sem("grow_ready")
        dequantised, sum_ready = sem("dequantised"), sem("sum_ready")
        fold_done, fold_copied = sem("fold_done"), sem("fold_copied")
        turned, turned_copied = sem("turned"), sem("turned_copied")
        op_ones, v_zeroed, v_set = sem("op_ones"), sem("v_zeroed"), sem("v_set")
        job_done, job_read = sem("job_done"), sem("job_read")
        form_ready, part1_ready, rest1_ready = sem("form_ready"), sem("part1_ready"), sem("rest1_ready")
        part2_ready, part3_ready = sem("part2_ready"), sem("part3_ready")
        rstd_ready = [sem(f"rstd_ready_{n}") for n in ("x", "y", "x1", "f")]
        ln_step = [sem(f"ln_step_{n}") for n in ("x", "y", "x1", "f")]
        x1_ready = sem("x1_ready")
        tanh_ready, out_ready = sem("tanh_ready"), sem("out_ready")
        rowscore_ready, rowscore_used = sem("rowscore_ready"), sem("rowscore_used")
        neg1_ready, rest_ready, neg2_ready, neg3_ready = sem("neg1_ready"), sem("rest_ready"), sem("neg2_ready"), sem("neg3_ready")
        score_ready, fixed, shifted = sem("score_ready"), sem("fixed"), sem("shifted")
        exp_done, pv_done, o_copied = sem("exp_done"), sem("pv_done"), sem("o_copied")
        den_ready = sem("den_ready")

        passed = {e: sem(f"passed_{e}") for e in ("sp", "dve", "pool")}

        def wait_alone(eng, name, awaited, n):
            if isinstance(n, int):
                wait(eng, awaited, n)
            else:
                eng.wait_ge(awaited, n).then_inc(passed[name], 1)

        DMAS_IN = 4 * len(Q_PART)
        block = ctx.enter_context(nc.Block())

        def over_phases(phase):
            def engine(eng):
                phase(eng, -1, 1)
                phase(eng, 0, 0)
                with eng.Fori(0, (B - 2) // 2) as i:
                    phase(eng, i * 2 + 1, 1)
                    phase(eng, i * 2 + 2, 0)
                phase(eng, B - 1, 1)
                phase(eng, B, 0)
            return engine

        def batch_of(dram, b):
            return dram[bass.ds(b, 1)].rearrange("a p t d -> p (a t) d")

        def sync_phase(sp, p, par):
            pre, att, post = runs(p)
            j = p + 1
            nxt = 1 - par
            if post:
                wait_alone(sp, "sp", x1_ready, p - 1)
                sp.dma_start(x_res[:], batch_of(x_tiles, p - 1)).then_inc(xres_loaded, 16)
            if pre:
                wait_alone(sp, "sp", ln_step[0], 4 * j)
                sp.dma_start(x_in[:], batch_of(x_tiles, j)).then_inc(x_loaded, 16)
                wait_alone(sp, "sp", operands_in, 16 * DMAS_IN * j)
                for half in range(2):
                    wait_alone(sp, "sp", part3_ready, 2 * j + half + 1)
                    sp.dma_start(spill[:, :, 2 * half:2 * half + 2, :],
                                 parts[:, :, 2 * half:2 * half + 2, :]).then_inc(spilled, 16)
                    if half == 0:
                        wait_alone(sp, "sp", shifted, SLOTS * (j - 1))
                        wait_alone(sp, "sp", op_ones, 2)
                    wait_alone(sp, "sp", spilled, 16 * (2 * j + half + 1))
                    for s in range(len(Q_PART)):
                        for form in (QA, QB) if half == 0 else (KA, KB):
                            op = (q_op, q_op, ka_op, kb_op)[form][nxt]
                            row = HD * s + (ROWS if form in (QB, KB) else 0)
                            part = (Q_PART if half == 0 else K_PART)[s]
                            sp.dma_start(op[row:row + HD],
                                         spill[:, part, form, :].rearrange("(h d) t -> d h t", d=HD)
                                         ).then_inc(operands_in, 16)
            if post:
                wait_alone(sp, "sp", out_ready, p)
                sp.dma_start(batch_of(out_tiles, p - 1), x1[:]).then_inc(stored, 16)

        @block.sync
        def _(sp):
            for dst, src in ((wkv[:, 0, :], w_k), (wkv[:, 1, :], w_v), (wd_sb[:], w_dkv), (wup[:, 0, :], w_uk),
                             (wup[:, 1, :], w_uv), (wq_sb[:], w_q), (wo_sb[:], w_o),
                             (w_int[0], w_gate.rearrange("(j p) d -> p j d", p=P)),
                             (w_int[1], w_up.rearrange("(j p) d -> p j d", p=P)),
                             (w_int[2], w_down.rearrange("d (j p) -> d j p", p=P))):
                sp.dma_start(dst, src).then_inc(w_loaded, 16)
            over_phases(sync_phase)(sp)
            sp.wait_ge(stored, 16 * B)
            sp.wait_ge(spilled, 16 * 2 * B)

        def pe_phase(pe, p, par):
            pre, att, post = runs(p)
            j, nxt = p + 1, 1 - par
            todo = jobs(p)

            def scores(n):
                g, kt, pair = n // GS, n % GS // 2, n % 2
                if n == 0:
                    pe.wait_ge(operands_in, 16 * DMAS_IN * (p + 1))
                if n % GS == 0:
                    pe.wait_ge(max_in, 16 * 3 * (p * NG + g + 1))
                wait(pe, exp_done, SLOTS * p + n - 1)
                for i in range(2):
                    h = g * HG + 2 * pair + i
                    keys = slice(P * kt, P * kt + P)
                    bank = score[:, n % 2, i, :]
                    if kt < T - 1:
                        pe.matmul(bank[:, P * kt + P:S], ka_op[par][0:ALL_ROWS, h, keys],
                                  q_op[par][0:ALL_ROWS, h, P * kt + P:S], start=True, stop=True, skip_group_check=True)
                    if kt > 0:
                        pe.matmul(bank[:, 0:P * kt], kb_op[par][0:ALL_ROWS, h, keys],
                                  q_op[par][0:ALL_ROWS, h, 0:P * kt], start=True, stop=True, skip_group_check=True)
                    mm = pe.matmul(bank[:, keys], ka_op[par][0:MAX_ROW, h, keys], q_op[par][0:MAX_ROW, h, keys],
                                   start=True, stop=False, skip_group_check=True)
                mm.then_inc(score_ready, 1)

            def shift(n):
                g, kt, pair = n // GS, n % GS // 2, n % 2
                pe.wait_ge(fixed, SLOTS * p + n + 1)
                keys = slice(P * kt, P * kt + P)
                for i in range(2):
                    h = g * HG + 2 * pair + i
                    mm = pe.matmul(score[:, n % 2, i, keys], ka_op[par][MAX_ROW:ALL_ROWS, h, keys],
                                   q_op[par][MAX_ROW:ALL_ROWS, h, keys], start=False, stop=True, skip_group_check=True)
                mm.then_inc(shifted, 1)

            def row_scores(n):
                if not has_max(p, n):
                    return
                i0 = sum(MAX_TILES[:n % GS])
                mg = max_group(p, n)
                own = n // GS < NG - 1
                side, g = (par, n // GS + 1) if own else (nxt, 0)
                for i in range(i0, i0 + MAX_TILES[n % GS]):
                    if i == 0 and not own:
                        pe.wait_ge(operands_in, 16 * DMAS_IN * (j + 1))
                    wait(pe, rowscore_used, mg * HG * T + i - 1)
                    h, qt = g * HG + i // T, i % T
                    pe.matmul(rowscore[:, i % 2, :], q_op[side][0:MAX_ROW, h, P * qt:P * qt + P],
                              ka_op[side][0:MAX_ROW, h, :], start=True, stop=True).then_inc(rowscore_ready, 1)

            def weighted(n):
                g, kt = n // GS, n % GS // 2
                pe.wait_ge(exp_done, SLOTS * p + n + 2)
                if kt == 0:
                    wait(pe, o_copied, NG * p + g)
                for i in range(HG):
                    mm = pe.matmul(o_acc[32 * i:32 * i + 32, :], v_op[par][:, kt, g * HG + i, :],
                                   probs[:, (n + i // 2) % 4, i % 2, :], start=kt == 0, stop=kt == T - 1)
                mm.then_inc(pv_done, 1)

            def weighted_last():
                if not post:
                    return
                pe.wait_ge(exp_done, SLOTS * p)
                for i in range(HG):
                    mm = pe.matmul(o_acc[32 * i:32 * i + 32, :], v_op[nxt][:, T - 1, H - HG + i, :],
                                   probs[:, (SLOTS - 2 + i // 2) % 4, i % 2, :], start=False, stop=True)
                mm.then_inc(pv_done, 1)

            def turn(src):
                for t in range(T):
                    mm = pe.transpose(work[:, P * t:P * t + P], src(t), ident[:])
                return mm

            def job(kind, i, n):
                wait(pe, job_read, job_number(p, n) - 1)
                if kind == "xT":
                    pe.wait_ge(ln_step[0], 4 * (j + 1))
                    mm = turn(lambda t: xn[:, t, :])
                elif kind in "qk":
                    w = wq_sb[:] if kind == "q" else wkv_full[:, 0, :]
                    mm = pe.matmul(work[:], w, xn_t[:], start=True, stop=True)
                elif kind == "v":
                    for t in range(T):
                        mm = pe.matmul(work[:, P * t:P * t + P], xn_t[:, P * t:P * t + P], wkv_full[:, 1, :],
                                       start=True, stop=True)
                elif kind == "maxT":
                    pe.wait_ge(rowscore_used, HG * T * (max_group(p, n) + 1))
                    mm = pe.transpose(work[0:HG * T, 0:P], row_max[:], ident[:])
                elif kind == "oT":
                    pe.wait_ge(o_copied, NG * (p - 1 if i == 3 else p) + i + 1)
                    mm = turn(lambda t: o_sb[:, P * t:P * t + P])
                elif kind == "aT":
                    mm = turn(lambda t: attn[:, t, :])
                elif kind == "y":
                    for t in range(T):
                        mm = pe.matmul(work[:, P * t:P * t + P], attn_t[:, P * t:P * t + P], wo_sb[:],
                                       start=True, stop=True)
                elif kind == "x1T":
                    pe.wait_ge(ln_step[2], 4 * p)
                    mm = turn(lambda t: x1n[:, t, :])
                elif kind in ("gate", "up"):
                    mm = pe.matmul(work[:], wffn[:, 0 if kind == "gate" else 1, i, :], x1n_t[:], start=True, stop=True)
                else:
                    for t in range(T):
                        for k in range(J):
                            mm = pe.matmul(work[:, P * t:P * t + P], hid[:, k, P * t:P * t + P], wffn[:, 2, k, :],
                                           start=k == 0, stop=k == J - 1)
                mm.then_inc(job_done, 1)

            for n in range(SLOTS):
                if att:
                    scores(n)
                row_scores(n)
                if n in todo:
                    job(*todo[n], n)
                if att:
                    shift(n)
                if n == 0:
                    weighted_last()
                elif att and n % 2 == 0:
                    weighted(n - 2)

        @block.tensor
        def _(pe):
            pe.wait_ge(const_ready, 1)
            pe.wait_ge(sum_ready, 1)
            pe.transpose(score[:, 0, 0, 0:D], wkv[:, 0, :], ident[:]).then_inc(fold_done, 1)
            pe.wait_ge(fold_copied, 1)
            pe.matmul(score[0:DL, 0, 1, 0:D], wd_sb[:], wkv_sum_t[:], start=True, stop=True).then_inc(fold_done, 1)
            pe.wait_ge(fold_copied, 2)
            for i in range(2):
                mm = pe.matmul(score[:, 0, 0, D * i:D * i + D], lat_t[:], wup[:, i, :], start=True, stop=True)
            mm.then_inc(fold_done, 1)
            for m in range(3):
                pe.wait_ge(dequantised, m + 1)
                for k in range(J):
                    mm = pe.transpose(score[:, 1, m % 2, P * k:P * k + P] if m < 2 else o_acc[:, P * k:P * k + P],
                                      w_raw[:, m, P * k:P * k + P], ident[:])
                mm.then_inc(turned, 1)
            pe.wait_ge(fold_copied, 3)
            pe.wait_ge(turned_copied, 3)
            over_phases(pe_phase)(pe)

        def act_phase(act, p, par):
            pre, att, post = runs(p)
            j, nxt = p + 1, 1 - par
            todo = jobs(p)

            def first_part(half):
                f = slice(2 * half, 2 * half + 2)
                act.wait_ge(form_ready, 2 * j + half + 1)
                wait(act, spilled, 32 * j)
                nc.scalar.copy(parts[:, 0, f, :], forms[:, f, :]).then_inc(part1_ready, 1)

            def second_part(half):
                f = slice(2 * half, 2 * half + 2)
                act.wait_ge(rest1_ready, 2 * j + half + 1)
                nc.scalar.copy(parts[:, 1, f, :], forms[:, f, :]).then_inc(part2_ready, 1)

            for n in range(SLOTS):
                if att:
                    act.wait_ge(shifted, SLOTS * p + n + 1)
                    wait(act, pv_done, SLOTS // 2 * p + n // 2 - 1)
                    nc.scalar.activation(probs[:, n % 4], score[:, n % 2], ACT.Exp,
                                         scale=SCORE_SCALE).then_inc(exp_done, 1)
                if (post and n == 0) or (att and n and n % GS == 0):
                    act.wait_ge(pv_done, SLOTS // 2 * p + n // 2)
                    wait(act, job_done, job_number(p, n - 5) if n else job_number(p, 0))
                    nc.scalar.copy(o_sb[:], o_acc[:]).then_inc(o_copied, 1)
                if n % GS == GS - 1 and has_max(p, n):
                    own = n // GS < NG - 1
                    op, g = (q_op[par], n // GS + 1) if own else (q_op[nxt], 0)
                    act.wait_ge(neg3_ready, max_group(p, n) + 1)
                    for c in range(3):
                        act.dma_start(op[MAX_ROW + c:MAX_ROW + c + 1, g * HG:(g + 1) * HG, :]
                                      .rearrange("p h (q t) -> p (h q) t", q=T), neg_max[:, c, :]).then_inc(max_in, 16)
                if pre:
                    if n == 5:
                        first_part(0)
                    elif n == 7:
                        second_part(0)
                    elif n == 9:
                        first_part(1)
                    elif n == 12:
                        second_part(1)
                if n not in todo:
                    continue
                kind, i = todo[n]
                if kind in ("xT", "q", "k", "v", "aT", "x1T", "gate"):
                    act.wait_ge(job_done, job_number(p, n))
                if kind == "xT":
                    nc.scalar.copy(xn_t[:], work[:]).then_inc(job_read, 1)
                elif kind in ("q", "k"):
                    nc.scalar.copy(qk[:, 0 if kind == "q" else 1, :], work[:]).then_inc(job_read, 1)
                elif kind == "v":
                    wait(act, pv_done, SLOTS // 2 * (j - 1))
                    act.wait_ge(v_set, 2)
                    nc.scalar.copy(v_op[nxt][:, :, :, 0:HD],
                                   work[:].rearrange("p (t h d) -> p t h d", t=T, h=H)).then_inc(job_read, 1)
                elif kind == "aT":
                    nc.scalar.copy(attn_t[:], work[:]).then_inc(job_read, 1)
                elif kind == "x1T":
                    nc.scalar.copy(x1n_t[:], work[:]).then_inc(job_read, 1)
                elif kind == "gate":
                    nc.scalar.activation(th[:], work[:], ACT.Tanh, scale=0.5).then_inc(tanh_ready, 1)

        @block.scalar
        def _(act):
            act.wait_ge(exp_ready, 3)
            nc.scalar.activation(grow[:, 0, :], grow[:, 0, :], ACT.Exp, scale=-DECAY)
            nc.scalar.activation(grow[:, 2, :], grow[:, 2, :], ACT.Exp, scale=-DECAY)
            nc.scalar.activation(grow[:, 1, :], grow[:, 1, :], ACT.Exp, scale=DECAY)
            nc.scalar.activation(fix_row[:], fix_row[:], ACT.Exp, scale=2 * DECAY)
            nc.scalar.activation(fix_key[:], fix_key[:], ACT.Exp, scale=2 * DECAY).then_inc(grow_ready, 1)
            act.wait_ge(fold_done, 1)
            nc.scalar.copy(wkv_sum_t[:], score[:, 0, 0, 0:D]).then_inc(fold_copied, 1)
            act.wait_ge(fold_done, 2)
            nc.scalar.copy(lat_t[:], score[0:DL, 0, 1, 0:D]).then_inc(fold_copied, 1)
            act.wait_ge(fold_done, 3)
            nc.scalar.copy(wkv_full[:], score[:, 0, 0, 0:2 * D].rearrange("p (i d) -> p i d", i=2)).then_inc(fold_copied, 1)
            for m in range(3):
                act.wait_ge(turned, m + 1)
                src = score[:, 1, m, 0:HID] if m < 2 else o_acc[:, 0:HID]
                nc.scalar.copy(wffn[:, m], src.rearrange("p (j q) -> p j q", j=J)).then_inc(turned_copied, 1)
            over_phases(act_phase)(act)

        def dve_phase(dve, p, par):
            pre, att, post = runs(p)
            j = p + 1
            todo = jobs(p)

            def layer_norm(src, dst, which, b, done):
                step, st, mo, rs = ln_step[which], stats[which], moments[which], rstd[which]
                per = 4 if done is step else 3
                for t in range(T):
                    ins = nc.vector.bn_stats(st[:, t, :], src(t))
                ins.then_inc(step, 1)
                wait_alone(dve, "dve", step, per * b + 1)
                for t in range(T):
                    ins = nc.vector.bn_aggr(mo[:, t, :], st[:, t, :])
                ins.then_inc(step, 1)
                dve.wait_ge(step, per * b + 2)
                nc.vector.tensor_scalar(rs[:], mo[:, :, 1], EPS, None, ALU.add).then_inc(step, 1)
                dve.wait_ge(rstd_ready[which], b + 1)
                for t in range(T):
                    ins = nc.vector.tensor_scalar(dst[:, t, :], src(t), mo[:, t, 0:1], rs[:, t:t + 1],
                                                  ALU.subtract, ALU.mult)
                ins.then_inc(done, 1)

            def fix(n):
                kt = n % GS // 2
                dve.wait_ge(score_ready, SLOTS * p + n + 1)
                block_ = score[:, n % 2, :, P * kt:P * kt + P]
                nc.vector.tensor_tensor(block_, block_, fix_key[:, None, :].broadcast_to([P, 2, P]),
                                        ALU.mult).then_inc(fixed, 1)

            def maxima(n):
                if not has_max(p, n):
                    return
                i0, mg = sum(MAX_TILES[:n % GS]), max_group(p, n)
                for i in range(i0, i0 + MAX_TILES[n % GS]):
                    wait_alone(dve, "dve", rowscore_ready, mg * HG * T + i + 1)
                    nc.vector.tensor_tensor_reduce(out=max_junk[:, i % 2, :], in0=rowscore[:, i % 2, :], in1=fix_row[:, P * (T - 1 - i % T):P * (T - 1 - i % T) + S],
                                                   scale=1.0, scalar=-3.0e38, op0=ALU.mult, op1=ALU.max,
                                                   accum_out=row_max[:, i:i + 1]).then_inc(rowscore_used, 1)

            def heads_out(g, done_groups):
                sums = work[:].rearrange("p (t i c) -> p t i c", t=T, i=HG)
                nc.vector.reciprocal(den[:], sums[:, :, :, HD]).then_inc(den_ready, 1)
                dve.wait_ge(den_ready, done_groups + 1)
                dst = attn[:, :, g * HG * HD:(g + 1) * HG * HD].rearrange("p t (i d) -> p t i d", i=HG)
                nc.vector.tensor_tensor(dst, sums[:, :, :, 0:HD], den[:, :, :, None].broadcast_to([P, T, HG, HD]),
                                        ALU.mult).then_inc(job_read, 1)

            def tile(buf):
                return lambda t: buf[:, P * t:P * t + P]

            for n in range(SLOTS):
                if att:
                    fix(n)
                maxima(n)
                if pre and n == 0:
                    dve.wait_ge(x_loaded, 16 * (j + 1))
                    wait(dve, job_done, job_number(p, 0))
                    layer_norm(lambda t: x_in[:, t, :], xn, 0, j, ln_step[0])
                if post and n == 9:
                    dve.wait_ge(x1_ready, p)
                    layer_norm(lambda t: x1[:, t, :], x1n, 2, p - 1, ln_step[2])
                if n not in todo:
                    continue
                kind, i = todo[n]
                number = job_number(p, n)
                if kind in ("maxT", "oT", "y", "up", "down"):
                    dve.wait_ge(job_done, number)
                if kind == "maxT":
                    mg = max_group(p, n)
                    raw = work[0:HG * T, 0:P]
                    wait(dve, max_in, 48 * mg)
                    nc.vector.tensor_scalar(neg_max[:, 0, :], raw, -1.0, None, ALU.mult).then_inc(neg1_ready, 1)
                    dve.wait_ge(neg1_ready, mg + 1)
                    nc.vector.scalar_tensor_tensor(out=max_rest[:], in0=raw, scalar=-1.0, in1=neg_max[:, 0, :],
                                                   op0=ALU.mult, op1=ALU.subtract).then_inc(job_read, 1)
                elif kind == "oT":
                    heads_out(i, NG * (p - 1 if i == 3 else p) + i)
                elif kind == "y":
                    layer_norm(tile(work), yn, 1, p - 1, job_read)
                elif kind == "gate":
                    dve.wait_ge(tanh_ready, J * (p - 1) + i + 1)
                    nc.vector.scalar_tensor_tensor(out=th[:], in0=th[:], scalar=1.0, in1=work[:],
                                                   op0=ALU.add, op1=ALU.mult).then_inc(job_read, 1)
                elif kind == "up":
                    dve.wait_ge(job_read, number - 1)
                    nc.vector.tensor_tensor(hid[:, i, :], th[:], work[:], ALU.mult).then_inc(job_read, 1)
                elif kind == "down":
                    layer_norm(tile(work), yn, 3, p - 1, job_read)

        @block.vector
        def _(dve):
            dve.wait_ge(w_loaded, 16 * 10)
            nc.vector.tensor_tensor(wkv[:, 0, :], wkv[:, 0, :], wkv[:, 1, :], ALU.add).then_inc(sum_ready, 1)
            for m in range(3):
                nc.vector.tensor_scalar(w_raw[:, m, :].rearrange("p (j d) -> p j d", j=J), w_int[m], DEQUANT,
                                        0.5 if m == 2 else 1.0, ALU.mult, ALU.mult).then_inc(dequantised, 1)
            dve.wait_ge(const_ready, 3)
            nc.vector.tensor_scalar(fix_row[:], fix_row[:], 0.0, None, ALU.min).then_inc(exp_ready, 1)
            nc.vector.tensor_scalar(fix_key[:], fix_key[:], 0.0, None, ALU.min).then_inc(exp_ready, 1)
            for i in range(2):
                nc.vector.memset(ka_op[i][0:MAX_ROW].rearrange("p h t -> p (h t)").bitcast(F32), 0.0)
                nc.vector.memset(kb_op[i][0:MAX_ROW].rearrange("p h t -> p (h t)").bitcast(F32), 0.0)
                nc.vector.memset(ka_op[i][MAX_ROW:ALL_ROWS], 1.0)
                nc.vector.memset(kb_op[i][MAX_ROW:ALL_ROWS], 1.0).then_inc(op_ones, 1)
            dve.wait_ge(grow_ready, 1)
            over_phases(dve_phase)(dve)

        def pool_phase(pool, p, par):
            pre, att, post = runs(p)
            j = p + 1

            def form(half):
                f = slice(2 * half, 2 * half + 2)
                pool.wait_ge(job_read, job_number(p, 5 if half else 2))
                wait(pool, part3_ready, 2 * j)
                nc.gpsimd.tensor_tensor(forms[:, f, :], qk[:, half:half + 1, :].broadcast_to([P, 2, S]),
                                        grow[:, half and 1 or 0:(half and 1 or 0) + 2, :],
                                        ALU.mult).then_inc(form_ready, 1)

            def rest(half):
                f = slice(2 * half, 2 * half + 2)
                pool.wait_ge(part1_ready, 2 * j + half + 1)
                nc.gpsimd.tensor_tensor(forms[:, f, :], forms[:, f, :], parts[:, 0, f, :],
                                        ALU.subtract).then_inc(rest1_ready, 1)

            def third_part(half):
                f = slice(2 * half, 2 * half + 2)
                pool.wait_ge(part2_ready, 2 * j + half + 1)
                nc.gpsimd.tensor_tensor(parts[:, 2, f, :], forms[:, f, :], parts[:, 1, f, :],
                                        ALU.subtract).then_inc(part3_ready, 1)

            def inverse_root(which, b):
                pool.wait_ge(ln_step[which], (4 if which in (0, 2) else 3) * b + 3)
                nc.gpsimd.tensor_tensor(rstd[which][:], rstd[which][:], minus_half[:], ALU.pow).then_inc(rstd_ready[which], 1)

            for n in range(SLOTS):
                if pre and n == 0:
                    inverse_root(0, j)
                if pre and n == 3:
                    form(0)
                if pre and n == 5:
                    rest(0)
                if n % GS == 6 and has_max(p, n):
                    mg = max_group(p, n)
                    wait_alone(pool, "pool", job_read, job_number(p, n))
                    nc.gpsimd.tensor_copy(neg_max[:, 1, :], max_rest[:]).then_inc(neg2_ready, 1)
                    pool.wait_ge(neg2_ready, mg + 1)
                    nc.gpsimd.tensor_tensor(neg_max[:, 2, :], max_rest[:], neg_max[:, 1, :],
                                            ALU.subtract).then_inc(neg3_ready, 1)
                if pre and n == 6:
                    form(1)
                if post and n == 8:
                    inverse_root(1, p - 1)
                    pool.wait_ge(xres_loaded, 16 * p)
                    pool.wait_ge(job_read, job_number(p, 8))
                    wait(pool, stored, 16 * (p - 1))
                    nc.gpsimd.tensor_tensor(x1[:], yn[:], x_res[:], ALU.add).then_inc(x1_ready, 1)
                if post and n == 9:
                    inverse_root(2, p - 1)
                if pre and n == 10:
                    rest(1)
                if pre and n == 11:
                    third_part(0)
                if pre and n == 13:
                    third_part(1)
                if post and n == 21:
                    inverse_root(3, p - 1)
                    pool.wait_ge(job_read, job_number(p, 21))
                    nc.gpsimd.tensor_tensor(x1[:], yn[:], x1[:], ALU.add).then_inc(out_ready, 1)

        @block.gpsimd
        def _(pool):
            nc.gpsimd.memset(minus_half[:], -0.5)
            nc.gpsimd.memset(ident[:], 0.0).then_inc(v_zeroed, 1)
            pool.wait_ge(v_zeroed, 1)
            nc.gpsimd.affine_select(out=ident[:], in_=ident[:], compare_op=ALU.not_equal, fill=1.0, base=0,
                                    pattern=[[-1, P]], channel_multiplier=1).then_inc(const_ready, 1)
            nc.gpsimd.iota(fix_row[:], pattern=[[-1, S + (T - 1) * P]], base=(T - 1) * P, channel_multiplier=1,
                           allow_small_or_imprecise_dtypes=True).then_inc(const_ready, 1)
            nc.gpsimd.iota(fix_key[:], pattern=[[1, P]], base=0, channel_multiplier=-1,
                           allow_small_or_imprecise_dtypes=True).then_inc(const_ready, 1)
            nc.gpsimd.iota(grow[:], pattern=[[0, 3], [1, S]], base=-(S // 2), channel_multiplier=0,
                           allow_small_or_imprecise_dtypes=True).then_inc(exp_ready, 1)
            for i in range(2):
                nc.gpsimd.memset(v_op[i][:], 0.0).then_inc(v_zeroed, 1)
                pool.wait_ge(v_zeroed, i + 2)
                nc.gpsimd.memset(v_op[i][:, :, :, HD:HD + 1], 1.0).then_inc(v_set, 1)
            pool.wait_ge(grow_ready, 1)
            pool.wait_ge(turned, 3)
            over_phases(pool_phase)(pool)


INPUTS = ("L0_attn_x", "L0_attn_W_q", "L0_attn_W_k", "L0_attn_W_v", "L0_attn_W_o", "L0_attn_W_down_kv",
          "L0_attn_W_up_k", "L0_attn_W_up_v", "L0_ffn_w_gate", "L0_ffn_w_up", "L0_ffn_w_down")


def kernel(**inputs):
    import numpy as np
    import concourse.bacc as bacc
    from concourse.bass_utils import run_bass_kernel_spmd

    nc = bacc.Bacc("TRN2", target_bir_lowering=False, num_devices=1)
    arrays, args = {}, []
    for name in INPUTS:
        a = np.ascontiguousarray(inputs[name])
        arrays[name] = a
        args.append(nc.dram_tensor(name, a.shape, mybir.dt.from_np(a.dtype), kind="ExternalInput").ap())
    out = nc.dram_tensor("out", (B, S, D), F32, kind="ExternalOutput").ap()
    sandwich(nc, *args, out)
    result = run_bass_kernel_spmd(nc, [arrays], core_ids=[0])
    return result.results[0]["out"]
```

```python
from contextlib import ExitStack

import concourse.bass as bass
from concourse import mybir

F32 = mybir.dt.float32
BF16 = mybir.dt.bfloat16
I32 = mybir.dt.int32
ALU = mybir.AluOpType
ACT = mybir.ActivationFunctionType

B, S, D = 8, 512, 128
H, HD, DL = 16, 8, 32
HID = 384
P = 128
T = S // P
J = HID // P
HG = 4
NG = H // HG
SLOTS = 2 * T * NG
GS = SLOTS // NG
DECAY = 0.01
SCORE_SCALE = 1.0 / float(D) ** 0.5
DEQUANT = 1.0 / 127.0
EPS = 1e-5
Q_PART = (0, 0, 0, 1, 1, 2)
K_PART = (0, 1, 2, 0, 1, 0)
ROWS = HD * len(Q_PART)
MAX_ROW = 2 * ROWS
ALL_ROWS = MAX_ROW + 3
TWO_ONES = 0x3F803F80
QA, QB, KA, KB = range(4)

PRE = {2: ("xT", 0), 3: ("q", 0), 5: ("k", 0), 10: ("v", 0), 28: ("maxT", 4)}
ATT = {4: ("maxT", 1), 12: ("maxT", 2), 20: ("maxT", 3), 9: ("oT", 0), 19: ("oT", 1), 27: ("oT", 2)}
POST = {1: ("oT", 3), 6: ("aT", 0), 7: ("y", 0), 13: ("x1T", 0), 14: ("gate", 0), 16: ("up", 0),
        17: ("gate", 1), 21: ("up", 1), 22: ("gate", 2), 24: ("up", 2), 25: ("down", 0)}
SLOT = {job: slot for part in (PRE, ATT, POST) for slot, job in part.items()}
LEAD = 12
MAX_TILES = 2


def started(n):
    return max(n, 0) if isinstance(n, int) else n


def runs(p):
    if not isinstance(p, int):
        return True, True, True
    return p + 1 < B, 0 <= p < B, p >= 1


def jobs(p):
    pre, att, post = runs(p)
    return {**(PRE if pre else {}), **(ATT if att else {}), **(POST if post else {})}


def job_number(p, slot):
    def whole(n):
        return min(n, B) if isinstance(n, int) else n
    before = len(PRE) * whole(p + 1) + len(ATT) * started(p) + len(POST) * started(p - 1)
    return before + sum(s <= slot for s in jobs(p))


def max_tiles(p, n):
    g, first = (n + LEAD) // GS, (n + LEAD) % GS * MAX_TILES
    pre, att, _ = runs(p)
    if not (pre if g >= NG else att):
        return g, ()
    return g, range(first, first + MAX_TILES)


def wait(eng, sem, n):
    if isinstance(n, int) and n <= 0:
        return
    eng.wait_ge(sem, n)


def sandwich(nc, x, w_q, w_k, w_v, w_o, w_dkv, w_uk, w_uv, w_gate, w_up, w_down, out):
    with ExitStack() as ctx:
        def sb(name, shape, dt=F32):
            return ctx.enter_context(nc.sbuf_tensor(name, shape, dt))

        def psum(name, shape):
            return ctx.enter_context(nc.psum_tensor(name, shape, F32))

        def sem(name):
            return ctx.enter_context(nc.semaphore(name))

        spill = nc.dram_tensor("qk_parts", (4, 3, P, S), BF16, kind="Internal").ap()

        score = psum("score", [P, 2, 2, S])
        rowscore = psum("rowscore", [P, 2, S])
        o_acc = psum("o_acc", [P, S])
        work = psum("work", [P, S])

        q_op = [sb(f"q_op{i}", [P, H, S], BF16) for i in range(2)]
        ka_op = [sb(f"ka_op{i}", [P, H, S], BF16) for i in range(2)]
        kb_op = [sb(f"kb_op{i}", [P, H, S], BF16) for i in range(2)]
        v_op = [sb(f"v_op{i}", [P, T, H, 32]) for i in range(2)]
        probs = sb("probs", [P, 4, 2, S])
        forms = sb("forms", [P, 4, S])
        parts = sb("parts", [P, 3, 4, S], BF16)
        qk = sb("qk", [P, 2, S])
        x_in = sb("x_in", [P, T, D])
        x_res = sb("x_res", [P, T, D])
        xn = sb("xn", [P, T, D])
        xn_t = sb("xn_t", [P, S])
        o_sb = sb("o_sb", [P, S])
        attn = sb("attn", [P, T, D])
        yn = sb("yn", [P, T, D])
        x1 = sb("x1", [P, T, D])
        x1n, x1n_t = x_res, xn_t
        th = sb("th", [P, S])
        attn_t = th
        hid = sb("hid", [P, J, S])
        row_max = sb("row_max", [P, 2, HG * T])
        max_junk = sb("max_junk", [P, 2, S], BF16)
        neg_max = sb("neg_max", [HG * T, 3, P], BF16)
        max_rest = sb("max_rest", [HG * T, P])
        den = sb("den", [P, T, HG])
        stats = [sb(f"stats{i}", [P, T, 6]) for i in range(4)]
        moments = [sb(f"moments{i}", [P, T, 2]) for i in range(4)]
        rstd = [sb(f"rstd{i}", [P, T]) for i in range(4)]

        ident = sb("ident", [P, P])
        minus_half = sb("minus_half", [P, T])
        grow = sb("grow", [P, 3, S])
        fix_row = sb("fix_row", [P, S + (T - 1) * P])
        fix_key = sb("fix_key", [P, P])
        wq_sb = sb("wq_sb", [P, D])
        wq_raw = attn[:, 0, :]
        wo_sb = sb("wo_sb", [P, D])
        wkv = sb("wkv", [P, 2, D])
        wd_sb = sb("wd_sb", [P, DL])
        wup = sb("wup", [DL, 2, D])
        wkv_sum_t = sb("wkv_sum_t", [P, D])
        lat_t = sb("lat_t", [DL, D])
        wkv_full = sb("wkv_full", [P, 2, D])
        w_int = xn[:, 0:J, :].bitcast(I32), x1n[:, 0:J, :].bitcast(I32), yn[:, 0:J, :].bitcast(I32)
        w_raw = forms[:, 0:3, 0:HID]
        wffn = sb("wffn", [P, 3, J, P])

        x_tiles = x.rearrange("b (t p) d -> b p t d", p=P)
        out_tiles = out.rearrange("b (t p) d -> b p t d", p=P)

        x_loaded, xres_loaded, stored = sem("x_loaded"), sem("xres_loaded"), sem("stored")
        w_loaded, spilled, operands_in, max_in = sem("w_loaded"), sem("spilled"), sem("operands_in"), sem("max_in")
        const_ready, exp_ready, grow_ready = sem("const_ready"), sem("exp_ready"), sem("grow_ready")
        dequantised, sum_ready = sem("dequantised"), sem("sum_ready")
        fold_done, fold_copied = sem("fold_done"), sem("fold_copied")
        turned, turned_copied = sem("turned"), sem("turned_copied")
        op_ones, v_zeroed, v_set = sem("op_ones"), sem("v_zeroed"), sem("v_set")
        job_done, job_read = sem("job_done"), sem("job_read")
        form_ready, part1_ready, rest1_ready = sem("form_ready"), sem("part1_ready"), sem("rest1_ready")
        part2_ready, part3_ready = sem("part2_ready"), sem("part3_ready")
        rstd_ready = [sem(f"rstd_ready_{n}") for n in ("x", "y", "x1", "f")]
        ln_step = [sem(f"ln_step_{n}") for n in ("x", "y", "x1", "f")]
        x1_ready = sem("x1_ready")
        tanh_ready, out_ready = sem("tanh_ready"), sem("out_ready")
        rowscore_ready, rowscore_used = sem("rowscore_ready"), sem("rowscore_used")
        neg1_ready, rest_ready, neg2_ready, neg3_ready = sem("neg1_ready"), sem("rest_ready"), sem("neg2_ready"), sem("neg3_ready")
        score_ready, fixed, shifted = sem("score_ready"), sem("fixed"), sem("shifted")
        exp_done, pv_done, o_copied = sem("exp_done"), sem("pv_done"), sem("o_copied")
        den_ready = sem("den_ready")

        passed = {e: sem(f"passed_{e}") for e in ("sp", "dve", "pool")}

        def wait_alone(eng, name, awaited, n):
            if isinstance(n, int):
                wait(eng, awaited, n)
            else:
                eng.wait_ge(awaited, n).then_inc(passed[name], 1)

        DMAS_IN = 4 * 3
        block = ctx.enter_context(nc.Block())

        def over_phases(phase):
            def engine(eng):
                phase(eng, -1, 1)
                phase(eng, 0, 0)
                with eng.Fori(0, (B - 2) // 2) as i:
                    phase(eng, i * 2 + 1, 1)
                    phase(eng, i * 2 + 2, 0)
                phase(eng, B - 1, 1)
                phase(eng, B, 0)
            return engine

        def batch_of(dram, b):
            return dram[bass.ds(b, 1)].rearrange("a p t d -> p (a t) d")

        def sync_phase(sp, p, par):
            pre, att, post = runs(p)
            j = p + 1
            nxt = 1 - par
            if post:
                wait_alone(sp, "sp", job_done, job_number(p - 1, SLOT["x1T", 0]) if not isinstance(p, int) or p > 1 else 0)
                sp.dma_start(x_res[:], batch_of(x_tiles, p - 1)).then_inc(xres_loaded, 16)
            if pre:
                wait_alone(sp, "sp", ln_step[0], 4 * j)
                sp.dma_start(x_in[:], batch_of(x_tiles, j)).then_inc(x_loaded, 16)
                wait_alone(sp, "sp", operands_in, 16 * DMAS_IN * j)
                for half in range(2):
                    wait_alone(sp, "sp", part3_ready, 2 * j + half + 1)
                    for form in (2 * half, 2 * half + 1):
                        sp.dma_start(spill[form].rearrange("c p t -> p c t"), parts[:, :, form, :]).then_inc(spilled, 16)
                    if half == 0:
                        wait_alone(sp, "sp", shifted, SLOTS * (j - 1))
                        wait_alone(sp, "sp", op_ones, 2)
                    wait_alone(sp, "sp", spilled, 32 * (2 * j + half + 1))
                    for form in (QA, QB) if half == 0 else (KA, KB):
                        op = (q_op, q_op, ka_op, kb_op)[form][nxt]
                        row = ROWS if form in (QB, KB) else 0
                        for n in (3, 2, 1):
                            if half:
                                src = spill[form, 0:n].rearrange("c (d h) t -> (c d) (h t)", d=HD)
                            else:
                                src = spill[form, 3 - n:4 - n].rearrange("c (d h) t -> c d (h t)", d=HD) \
                                    .broadcast_to([n, HD, H * S])
                            sp.dma_start(op[row:row + n * HD].rearrange("p h t -> p (h t)"), src).then_inc(operands_in, 16)
                            row += n * HD
            if post:
                wait_alone(sp, "sp", out_ready, p)
                sp.dma_start(batch_of(out_tiles, p - 1), x1[:]).then_inc(stored, 16)

        @block.sync
        def _(sp):
            for dst, src in ((wkv[:, 0, :], w_k), (wkv[:, 1, :], w_v), (wd_sb[:], w_dkv), (wup[:, 0, :], w_uk),
                             (wup[:, 1, :], w_uv), (wq_raw, w_q), (wo_sb[:], w_o),
                             (w_int[0], w_gate.rearrange("(j p) d -> p j d", p=P)),
                             (w_int[1], w_up.rearrange("(j p) d -> p j d", p=P)),
                             (w_int[2], w_down.rearrange("d (j p) -> d j p", p=P))):
                sp.dma_start(dst, src).then_inc(w_loaded, 16)
            over_phases(sync_phase)(sp)
            sp.wait_ge(stored, 16 * B)
            sp.wait_ge(spilled, 16 * 4 * B)

        def pe_phase(pe, p, par):
            pre, att, post = runs(p)
            j, nxt = p + 1, 1 - par
            todo = jobs(p)

            def scores(n):
                g, kt, pair = n // GS, n % GS // 2, n % 2
                if n == 0:
                    pe.wait_ge(operands_in, 16 * DMAS_IN * (p + 1))
                if n % GS == 0:
                    pe.wait_ge(max_in, 16 * 3 * (p * NG + g + 1))
                wait(pe, exp_done, SLOTS * p + n - 1)
                for i in range(2):
                    h = g * HG + 2 * pair + i
                    keys = slice(P * kt, P * kt + P)
                    bank = score[:, n % 2, i, :]
                    if kt < T - 1:
                        pe.matmul(bank[:, P * kt + P:S], ka_op[par][0:ALL_ROWS, h, keys],
                                  q_op[par][0:ALL_ROWS, h, P * kt + P:S], start=True, stop=True, skip_group_check=True)
                    if kt > 0:
                        pe.matmul(bank[:, 0:P * kt], kb_op[par][0:ALL_ROWS, h, keys],
                                  q_op[par][0:ALL_ROWS, h, 0:P * kt], start=True, stop=True, skip_group_check=True)
                    mm = pe.matmul(bank[:, keys], ka_op[par][0:MAX_ROW, h, keys], q_op[par][0:MAX_ROW, h, keys],
                                   start=True, stop=False, skip_group_check=True)
                mm.then_inc(score_ready, 1)

            def shift(n):
                g, kt, pair = n // GS, n % GS // 2, n % 2
                pe.wait_ge(fixed, SLOTS * p + n + 1)
                keys = slice(P * kt, P * kt + P)
                for i in range(2):
                    h = g * HG + 2 * pair + i
                    mm = pe.matmul(score[:, n % 2, i, keys], ka_op[par][MAX_ROW:ALL_ROWS, h, keys],
                                   q_op[par][MAX_ROW:ALL_ROWS, h, keys], start=False, stop=True, skip_group_check=True)
                mm.then_inc(shifted, 1)

            def row_scores(n):
                gg, tiles = max_tiles(p, n)
                side, g = (par if gg < NG else nxt), gg % NG
                for i in tiles:
                    if i == 0 and g == 0:
                        pe.wait_ge(operands_in, 16 * DMAS_IN * (j + 1))
                    wait(pe, rowscore_used, (NG * p + gg) * HG * T + i - 1)
                    h, qt = g * HG + i // T, i % T
                    pe.matmul(rowscore[:, i % 2, :], q_op[side][0:MAX_ROW, h, P * qt:P * qt + P],
                              ka_op[side][0:MAX_ROW, h, :], start=True, stop=True).then_inc(rowscore_ready, 1)

            def weighted(n):
                g, kt = n // GS, n % GS // 2
                pe.wait_ge(exp_done, SLOTS * p + n + 2)
                if kt == 0:
                    wait(pe, o_copied, NG * p + g)
                for i in range(HG):
                    mm = pe.matmul(o_acc[32 * i:32 * i + 32, :], v_op[par][:, kt, g * HG + i, :],
                                   probs[:, (n + i // 2) % 4, i % 2, :], start=kt == 0, stop=kt == T - 1)
                mm.then_inc(pv_done, 1)

            def weighted_last():
                if not post:
                    return
                pe.wait_ge(exp_done, SLOTS * p)
                for i in range(HG):
                    mm = pe.matmul(o_acc[32 * i:32 * i + 32, :], v_op[nxt][:, T - 1, H - HG + i, :],
                                   probs[:, (SLOTS - 2 + i // 2) % 4, i % 2, :], start=False, stop=True)
                mm.then_inc(pv_done, 1)

            def turn(src):
                for t in range(T):
                    mm = pe.transpose(work[:, P * t:P * t + P], src(t), ident[:])
                return mm

            def job(kind, i, n):
                wait(pe, job_read, job_number(p, n) - 1)
                if kind == "xT":
                    pe.wait_ge(ln_step[0], 4 * (j + 1))
                    mm = turn(lambda t: xn[:, t, :])
                elif kind in "qk":
                    w = wq_sb[:] if kind == "q" else wkv_full[:, 0, :]
                    mm = pe.matmul(work[:], w, xn_t[:], start=True, stop=True)
                elif kind == "v":
                    for t in range(T):
                        mm = pe.matmul(work[:, P * t:P * t + P], xn_t[:, P * t:P * t + P], wkv_full[:, 1, :],
                                       start=True, stop=True)
                elif kind == "maxT":
                    pe.wait_ge(rowscore_used, HG * T * (NG * p + i + 1))
                    mm = pe.transpose(work[0:HG * T, 0:P], row_max[:, i % 2, :], ident[:])
                elif kind == "oT":
                    pe.wait_ge(o_copied, NG * (p - 1 if i == 3 else p) + i + 1)
                    mm = turn(lambda t: o_sb[:, P * t:P * t + P])
                elif kind == "aT":
                    mm = turn(lambda t: attn[:, t, :])
                elif kind == "y":
                    for t in range(T):
                        mm = pe.matmul(work[:, P * t:P * t + P], attn_t[:, P * t:P * t + P], wo_sb[:],
                                       start=True, stop=True)
                elif kind == "x1T":
                    pe.wait_ge(ln_step[2], 4 * p)
                    mm = turn(lambda t: x1n[:, t, :])
                elif kind in ("gate", "up"):
                    mm = pe.matmul(work[:], wffn[:, 0 if kind == "gate" else 1, i, :], x1n_t[:], start=True, stop=True)
                else:
                    for t in range(T):
                        for k in range(J):
                            mm = pe.matmul(work[:, P * t:P * t + P], hid[:, k, P * t:P * t + P], wffn[:, 2, k, :],
                                           start=k == 0, stop=k == J - 1)
                mm.then_inc(job_done, 1)

            for n in range(SLOTS):
                if att:
                    scores(n)
                row_scores(n)
                if att:
                    shift(n)
                if n in todo:
                    job(*todo[n], n)
                if n == 0:
                    weighted_last()
                elif att and n % 2 == 0:
                    weighted(n - 2)

        @block.tensor
        def _(pe):
            pe.wait_ge(const_ready, 1)
            pe.wait_ge(sum_ready, 1)
            pe.transpose(score[:, 0, 0, 0:D], wkv[:, 0, :], ident[:]).then_inc(fold_done, 1)
            pe.wait_ge(fold_copied, 1)
            pe.matmul(score[0:DL, 0, 1, 0:D], wd_sb[:], wkv_sum_t[:], start=True, stop=True).then_inc(fold_done, 1)
            pe.wait_ge(fold_copied, 2)
            for i in range(2):
                mm = pe.matmul(score[:, 0, 0, D * i:D * i + D], lat_t[:], wup[:, i, :], start=True, stop=True)
            mm.then_inc(fold_done, 1)
            for m in range(3):
                pe.wait_ge(dequantised, m + 1)
                for k in range(J):
                    mm = pe.transpose(score[:, 1, m % 2, P * k:P * k + P] if m < 2 else o_acc[:, P * k:P * k + P],
                                      w_raw[:, m, P * k:P * k + P], ident[:])
                mm.then_inc(turned, 1)
            pe.wait_ge(fold_copied, 3)
            pe.wait_ge(turned_copied, 3)
            over_phases(pe_phase)(pe)

        def act_phase(act, p, par):
            pre, att, post = runs(p)
            j, nxt = p + 1, 1 - par
            todo = jobs(p)

            def first_part(half):
                f = slice(2 * half, 2 * half + 2)
                act.wait_ge(form_ready, 2 * j + half + 1)
                wait(act, spilled, 64 * j)
                nc.scalar.copy(parts[:, 0, f, :], forms[:, f, :]).then_inc(part1_ready, 1)

            def second_part(half):
                f = slice(2 * half, 2 * half + 2)
                act.wait_ge(rest1_ready, 2 * j + half + 1)
                nc.scalar.copy(parts[:, 1, f, :], forms[:, f, :]).then_inc(part2_ready, 1)

            for n in range(SLOTS):
                if att:
                    act.wait_ge(shifted, SLOTS * p + n + 1)
                    wait(act, pv_done, SLOTS // 2 * p + n // 2 - 1)
                    nc.scalar.activation(probs[:, n % 4], score[:, n % 2], ACT.Exp,
                                         scale=SCORE_SCALE).then_inc(exp_done, 1)
                if (post and n == 0) or (att and n and n % GS == 0):
                    act.wait_ge(pv_done, SLOTS // 2 * p + n // 2)
                    wait(act, job_done, job_number(p, SLOT["oT", n // GS - 2] if n > GS else 1 if n else 0))
                    nc.scalar.copy(o_sb[:], o_acc[:]).then_inc(o_copied, 1)
                if todo.get(n - 1, ("", 0))[0] == "maxT":
                    gg = todo[n - 1][1]
                    op, g = (q_op[par] if gg < NG else q_op[nxt]), gg % NG
                    act.wait_ge(neg3_ready, NG * p + gg + 1)
                    for c in range(3):
                        act.dma_start(op[MAX_ROW + c:MAX_ROW + c + 1, g * HG:(g + 1) * HG, :]
                                      .rearrange("p h (q t) -> p (h q) t", q=T), neg_max[:, c, :]).then_inc(max_in, 16)
                if pre:
                    if n == 6:
                        first_part(0)
                    elif n == 9:
                        second_part(0)
                    elif n == 8:
                        first_part(1)
                    elif n == 11:
                        second_part(1)
                if n not in todo:
                    continue
                kind, i = todo[n]
                if kind in ("xT", "q", "k", "v", "aT", "x1T", "gate"):
                    act.wait_ge(job_done, job_number(p, n))
                if kind == "xT":
                    nc.scalar.copy(xn_t[:], work[:]).then_inc(job_read, 1)
                elif kind in ("q", "k"):
                    nc.scalar.copy(qk[:, 0 if kind == "q" else 1, :], work[:]).then_inc(job_read, 1)
                elif kind == "v":
                    wait(act, pv_done, SLOTS // 2 * (j - 1))
                    act.wait_ge(v_set, 2)
                    nc.scalar.copy(v_op[nxt][:, :, :, 0:HD],
                                   work[:].rearrange("p (t h d) -> p t h d", t=T, h=H)).then_inc(job_read, 1)
                elif kind == "aT":
                    nc.scalar.copy(attn_t[:], work[:]).then_inc(job_read, 1)
                elif kind == "x1T":
                    nc.scalar.copy(x1n_t[:], work[:]).then_inc(job_read, 1)
                elif kind == "gate":
                    nc.scalar.activation(th[:], work[:], ACT.Tanh, scale=0.5).then_inc(tanh_ready, 1)

        @block.scalar
        def _(act):
            act.wait_ge(exp_ready, 3)
            nc.scalar.activation(grow[:, 0, :], grow[:, 0, :], ACT.Exp, scale=-DECAY)
            nc.scalar.activation(grow[:, 2, :], grow[:, 2, :], ACT.Exp, scale=-DECAY)
            nc.scalar.activation(grow[:, 1, :], grow[:, 1, :], ACT.Exp, scale=DECAY)
            nc.scalar.activation(fix_row[:], fix_row[:], ACT.Exp, scale=2 * DECAY)
            nc.scalar.activation(fix_key[:], fix_key[:], ACT.Exp, scale=2 * DECAY).then_inc(grow_ready, 1)
            act.wait_ge(fold_done, 1)
            nc.scalar.copy(wkv_sum_t[:], score[:, 0, 0, 0:D]).then_inc(fold_copied, 1)
            act.wait_ge(fold_done, 2)
            nc.scalar.copy(lat_t[:], score[0:DL, 0, 1, 0:D]).then_inc(fold_copied, 1)
            act.wait_ge(w_loaded, 16 * 10)
            nc.scalar.copy(wq_sb[:].rearrange("p (d h) -> p h d", h=H), wq_raw.rearrange("p (h d) -> p h d", h=H))
            act.wait_ge(fold_done, 3)
            nc.scalar.copy(wkv_full[:, 0, :].rearrange("p (d h) -> p h d", h=H),
                           score[:, 0, 0, 0:D].rearrange("p (h d) -> p h d", h=H))
            nc.scalar.copy(wkv_full[:, 1, :], score[:, 0, 0, D:2 * D]).then_inc(fold_copied, 1)
            for m in range(3):
                act.wait_ge(turned, m + 1)
                src = score[:, 1, m, 0:HID] if m < 2 else o_acc[:, 0:HID]
                nc.scalar.copy(wffn[:, m], src.rearrange("p (j q) -> p j q", j=J)).then_inc(turned_copied, 1)
            over_phases(act_phase)(act)

        def dve_phase(dve, p, par):
            pre, att, post = runs(p)
            j = p + 1
            todo = jobs(p)

            def norm_statistics(src, which, b):
                step, st, mo, rs = ln_step[which], stats[which], moments[which], rstd[which]
                per = 4 if which in (0, 2) else 3
                for t in range(T):
                    ins = nc.vector.bn_stats(st[:, t, :], src(t))
                ins.then_inc(step, 1)
                wait_alone(dve, "dve", step, per * b + 1)
                for t in range(T):
                    ins = nc.vector.bn_aggr(mo[:, t, :], st[:, t, :])
                ins.then_inc(step, 1)
                dve.wait_ge(step, per * b + 2)
                nc.vector.tensor_scalar(rs[:], mo[:, :, 1], EPS, None, ALU.add).then_inc(step, 1)

            def norm_apply(src, dst, which, b, done):
                mo, rs = moments[which], rstd[which]
                dve.wait_ge(rstd_ready[which], b + 1)
                for t in range(T):
                    ins = nc.vector.tensor_scalar(dst[:, t, :], src(t), mo[:, t, 0:1], rs[:, t:t + 1],
                                                  ALU.subtract, ALU.mult)
                ins.then_inc(done, 1)

            def fix(n):
                kt = n % GS // 2
                dve.wait_ge(score_ready, SLOTS * p + n + 1)
                block_ = score[:, n % 2, :, P * kt:P * kt + P]
                nc.vector.tensor_tensor(block_, block_, fix_key[:, None, :].broadcast_to([P, 2, P]),
                                        ALU.mult).then_inc(fixed, 1)

            def maxima(n):
                gg, tiles = max_tiles(p, n)
                for i in tiles:
                    wait_alone(dve, "dve", rowscore_ready, (NG * p + gg) * HG * T + i + 1)
                    first = P * (T - 1 - i % T)
                    nc.vector.tensor_tensor_reduce(out=max_junk[:, i % 2, :], in0=rowscore[:, i % 2, :],
                                                   in1=fix_row[:, first:first + S], scale=1.0, scalar=-3.0e38,
                                                   op0=ALU.mult, op1=ALU.max,
                                                   accum_out=row_max[:, gg % 2, i:i + 1]).then_inc(rowscore_used, 1)

            def heads_out(g, done_groups):
                sums = work[:].rearrange("p (t i c) -> p t i c", t=T, i=HG)
                nc.vector.reciprocal(den[:], sums[:, :, :, HD]).then_inc(den_ready, 1)
                dve.wait_ge(den_ready, done_groups + 1)
                dst = attn[:, :, g * HG * HD:(g + 1) * HG * HD].rearrange("p t (i d) -> p t i d", i=HG)
                nc.vector.tensor_tensor(dst, sums[:, :, :, 0:HD], den[:, :, :, None].broadcast_to([P, T, HG, HD]),
                                        ALU.mult).then_inc(job_read, 1)

            def tile(buf):
                return lambda t: buf[:, P * t:P * t + P]

            for n in range(SLOTS):
                if att:
                    fix(n)
                if pre and n == 1:
                    norm_apply(lambda t: x_in[:, t, :], xn, 0, j, ln_step[0])
                if post and n == 8:
                    norm_apply(tile(work), yn, 1, p - 1, job_read)
                if post and n == 11:
                    norm_apply(lambda t: x1[:, t, :], x1n, 2, p - 1, ln_step[2])
                if post and n == 26:
                    norm_apply(tile(work), yn, 3, p - 1, job_read)
                maxima(n)
                if pre and n == 0:
                    dve.wait_ge(x_loaded, 16 * (j + 1))
                    wait(dve, job_done, job_number(p, 0))
                    norm_statistics(lambda t: x_in[:, t, :], 0, j)
                if post and n == 10:
                    dve.wait_ge(x1_ready, p)
                    norm_statistics(lambda t: x1[:, t, :], 2, p - 1)
                if todo.get(n - 1, ("", 0))[0] == "gate":
                    dve.wait_ge(tanh_ready, J * (p - 1) + todo[n - 1][1] + 1)
                    nc.vector.scalar_tensor_tensor(out=th[:], in0=th[:], scalar=1.0, in1=work[:],
                                                   op0=ALU.add, op1=ALU.mult).then_inc(job_read, 1)
                if n not in todo:
                    continue
                kind, i = todo[n]
                number = job_number(p, n)
                if kind in ("maxT", "oT", "y", "up", "down"):
                    dve.wait_ge(job_done, number)
                if kind == "maxT":
                    mg = NG * p + i
                    raw = work[0:HG * T, 0:P]
                    wait(dve, max_in, 48 * mg)
                    nc.vector.tensor_scalar(neg_max[:, 0, :], raw, -1.0, None, ALU.mult).then_inc(neg1_ready, 1)
                    dve.wait_ge(neg1_ready, mg + 1)
                    nc.vector.scalar_tensor_tensor(out=max_rest[:], in0=raw, scalar=-1.0, in1=neg_max[:, 0, :],
                                                   op0=ALU.mult, op1=ALU.subtract).then_inc(job_read, 1)
                elif kind == "oT":
                    heads_out(i, NG * (p - 1 if i == 3 else p) + i)
                elif kind == "y":
                    norm_statistics(tile(work), 1, p - 1)
                elif kind == "up":
                    dve.wait_ge(job_read, number - 1)
                    nc.vector.tensor_tensor(hid[:, i, :], th[:], work[:], ALU.mult).then_inc(job_read, 1)
                elif kind == "down":
                    norm_statistics(tile(work), 3, p - 1)

        @block.vector
        def _(dve):
            dve.wait_ge(w_loaded, 16 * 10)
            nc.vector.tensor_tensor(wkv[:, 0, :], wkv[:, 0, :], wkv[:, 1, :], ALU.add).then_inc(sum_ready, 1)
            for m in range(3):
                nc.vector.tensor_scalar(w_raw[:, m, :].rearrange("p (j d) -> p j d", j=J), w_int[m], DEQUANT,
                                        0.5 if m == 2 else 1.0, ALU.mult, ALU.mult).then_inc(dequantised, 1)
            dve.wait_ge(const_ready, 3)
            nc.vector.tensor_scalar(fix_row[:], fix_row[:], 0.0, None, ALU.min).then_inc(exp_ready, 1)
            nc.vector.tensor_scalar(fix_key[:], fix_key[:], 0.0, None, ALU.min).then_inc(exp_ready, 1)
            for i in range(2):
                nc.vector.memset(ka_op[i][0:MAX_ROW].rearrange("p h t -> p (h t)").bitcast(F32), 0.0)
                nc.vector.memset(kb_op[i][0:MAX_ROW].rearrange("p h t -> p (h t)").bitcast(F32), 0.0)
                for op in (ka_op, kb_op):
                    ins = nc.vector.memset(op[i][MAX_ROW:ALL_ROWS].rearrange("p h t -> p (h t)").bitcast(I32), TWO_ONES)
                ins.then_inc(op_ones, 1)
            dve.wait_ge(grow_ready, 1)
            over_phases(dve_phase)(dve)

        def pool_phase(pool, p, par):
            pre, att, post = runs(p)
            j = p + 1
            todo = jobs(p)

            def form(half):
                f = slice(2 * half, 2 * half + 2)
                pool.wait_ge(job_read, job_number(p, SLOT["k" if half else "q", 0]))
                wait(pool, part3_ready, 2 * j)
                nc.gpsimd.tensor_tensor(forms[:, f, :], qk[:, half:half + 1, :].broadcast_to([P, 2, S]),
                                        grow[:, half and 1 or 0:(half and 1 or 0) + 2, :],
                                        ALU.mult).then_inc(form_ready, 1)

            def rest(half):
                f = slice(2 * half, 2 * half + 2)
                pool.wait_ge(part1_ready, 2 * j + half + 1)
                nc.gpsimd.tensor_tensor(forms[:, f, :], forms[:, f, :], parts[:, 0, f, :],
                                        ALU.subtract).then_inc(rest1_ready, 1)

            def third_part(half):
                f = slice(2 * half, 2 * half + 2)
                pool.wait_ge(part2_ready, 2 * j + half + 1)
                nc.gpsimd.tensor_tensor(parts[:, 2, f, :], forms[:, f, :], parts[:, 1, f, :],
                                        ALU.subtract).then_inc(part3_ready, 1)

            def inverse_root(which, b):
                pool.wait_ge(ln_step[which], (4 if which in (0, 2) else 3) * b + 3)
                nc.gpsimd.tensor_tensor(rstd[which][:], rstd[which][:], minus_half[:], ALU.pow).then_inc(rstd_ready[which], 1)

            for n in range(SLOTS):
                if pre and n == 0:
                    inverse_root(0, j)
                if n in todo and todo[n][0] == "maxT":
                    mg = NG * p + todo[n][1]
                    wait_alone(pool, "pool", job_read, job_number(p, n))
                    nc.gpsimd.tensor_copy(neg_max[:, 1, :], max_rest[:]).then_inc(neg2_ready, 1)
                    pool.wait_ge(neg2_ready, mg + 1)
                    nc.gpsimd.tensor_tensor(neg_max[:, 2, :], max_rest[:], neg_max[:, 1, :],
                                            ALU.subtract).then_inc(neg3_ready, 1)
                if pre and n == 4:
                    form(0)
                if pre and n == 6:
                    form(1)
                if pre and n == 7:
                    rest(0)
                if post and n == 7:
                    inverse_root(1, p - 1)
                if post and n == 8:
                    pool.wait_ge(xres_loaded, 16 * p)
                    pool.wait_ge(job_read, job_number(p, SLOT["y", 0]))
                    wait(pool, stored, 16 * (p - 1))
                    nc.gpsimd.tensor_tensor(x1[:], yn[:], x_res[:], ALU.add).then_inc(x1_ready, 1)
                if pre and n == 9:
                    rest(1)
                if post and n == 10:
                    inverse_root(2, p - 1)
                if pre and n == 10:
                    third_part(0)
                if pre and n == 11:
                    third_part(1)
                if post and n == 25:
                    inverse_root(3, p - 1)
                if post and n == 26:
                    pool.wait_ge(job_read, job_number(p, SLOT["down", 0]))
                    nc.gpsimd.tensor_tensor(x1[:], yn[:], x1[:], ALU.add).then_inc(out_ready, 1)

        @block.gpsimd
        def _(pool):
            nc.gpsimd.memset(minus_half[:], -0.5)
            nc.gpsimd.memset(ident[:], 0.0).then_inc(v_zeroed, 1)
            pool.wait_ge(v_zeroed, 1)
            nc.gpsimd.affine_select(out=ident[:], in_=ident[:], compare_op=ALU.not_equal, fill=1.0, base=0,
                                    pattern=[[-1, P]], channel_multiplier=1).then_inc(const_ready, 1)
            nc.gpsimd.iota(fix_row[:], pattern=[[-1, S + (T - 1) * P]], base=(T - 1) * P, channel_multiplier=1,
                           allow_small_or_imprecise_dtypes=True).then_inc(const_ready, 1)
            nc.gpsimd.iota(fix_key[:], pattern=[[1, P]], base=0, channel_multiplier=-1,
                           allow_small_or_imprecise_dtypes=True).then_inc(const_ready, 1)
            nc.gpsimd.iota(grow[:], pattern=[[0, 3], [1, S]], base=-(S // 2), channel_multiplier=0,
                           allow_small_or_imprecise_dtypes=True).then_inc(exp_ready, 1)
            for i in range(2):
                nc.gpsimd.memset(v_op[i][:], 0.0).then_inc(v_zeroed, 1)
                pool.wait_ge(v_zeroed, i + 2)
                nc.gpsimd.memset(v_op[i][:, :, :, HD:HD + 1], 1.0).then_inc(v_set, 1)
            pool.wait_ge(grow_ready, 1)
            pool.wait_ge(turned, 3)
            over_phases(pool_phase)(pool)


INPUTS = ("L0_attn_x", "L0_attn_W_q", "L0_attn_W_k", "L0_attn_W_v", "L0_attn_W_o", "L0_attn_W_down_kv",
          "L0_attn_W_up_k", "L0_attn_W_up_v", "L0_ffn_w_gate", "L0_ffn_w_up", "L0_ffn_w_down")


def kernel(**inputs):
    import numpy as np
    import concourse.bacc as bacc
    from concourse.bass_utils import run_bass_kernel_spmd

    nc = bacc.Bacc("TRN2", target_bir_lowering=False, num_devices=1)
    arrays, args = {}, []
    for name in INPUTS:
        a = np.ascontiguousarray(inputs[name])
        arrays[name] = a
        args.append(nc.dram_tensor(name, a.shape, mybir.dt.from_np(a.dtype), kind="ExternalInput").ap())
    out = nc.dram_tensor("out", (B, S, D), F32, kind="ExternalOutput").ap()
    sandwich(nc, *args, out)
    result = run_bass_kernel_spmd(nc, [arrays], core_ids=[0])
    return result.results[0]["out"]
```

```python
from contextlib import ExitStack

import concourse.bass as bass
from concourse import mybir

F32 = mybir.dt.float32
BF16 = mybir.dt.bfloat16
I32 = mybir.dt.int32
ALU = mybir.AluOpType
ACT = mybir.ActivationFunctionType

B, S, D = 8, 512, 128
H, HD, DL = 16, 8, 32
HID = 384
P = 128
T = S // P
J = HID // P
HG = 4
NG = H // HG
SLOTS = 2 * T * NG
GS = SLOTS // NG
DECAY = 0.01
SCORE_SCALE = 1.0 / float(D) ** 0.5
DEQUANT = 1.0 / 127.0
EPS = 1e-5
Q_PART = (0, 0, 0, 1, 1, 2)
K_PART = (0, 1, 2, 0, 1, 0)
ROWS = HD * len(Q_PART)
MAX_ROW = 2 * ROWS
ALL_ROWS = MAX_ROW + 3
TWO_ONES = 0x3F803F80
QA, QB, KA, KB = range(4)

PRE = ((0, "xT", 0), (1, "q", 0), (3, "k", 0), (7, "v", 0), (27.5, "maxT", 4))
ATT = ((3.5, "maxT", 1), (11.5, "maxT", 2), (19.5, "maxT", 3), (9, "oT", 0), (18, "oT", 1), (26, "oT", 2))
POST = ((2, "oT", 3), (4, "aT", 0), (5, "y", 0), (13, "x1T", 0), (15, "gate", 0), (16, "gate", 1), (17, "up", 0),
        (19, "gate", 2), (21, "up", 1), (23, "up", 2),
        (24, "down", 0), (25, "down", 1), (27, "down", 2), (29, "down", 3))
SPLIT_STEPS = ((("form", 0), 2), (("form", 1), 4), (("rest", 0), 5), (("rest", 1), 7),
               (("third", 0), 9), (("third", 1), 10))
SPLIT_STEPS_0 = ((("form", 0), 1), (("rest", 0), 2), (("form", 1), 3), (("third", 0), 6),
                 (("rest", 1), 7), (("third", 1), 8))
LEAD = 12
MAX_TILES = 2


def started(n):
    return max(n, 0) if isinstance(n, int) else n


def runs(p):
    if not isinstance(p, int):
        return True, True, True
    return 0 <= p + 1 < B, 0 <= p < B, p >= 1


def ends(p):
    return isinstance(p, int) and p == B


def normalises(p):
    return not isinstance(p, int) or p + 2 < B


def jobs(p):
    pre, att, post = runs(p)
    return sorted(((PRE if pre else ()) + (ATT if att else ()) + (POST if post else ())), key=lambda job: job[0])


def jobs_of(p, n):
    return [(kind, i) for slot, kind, i in jobs(p) if slot == n]


def job_number(p, kind, i=0):
    def whole(n):
        return min(n, B) if isinstance(n, int) else n
    before = len(PRE) * whole(p + 1) + len(ATT) * started(p) + len(POST) * started(p - 1)
    return before + [(k, m) for _, k, m in jobs(p)].index((kind, i)) + 1


def max_tiles(p, n):
    g, first = (n + LEAD) // GS, (n + LEAD) % GS * MAX_TILES
    pre, att, _ = runs(p)
    if not (pre if g >= NG else att):
        return g, ()
    return g, range(first, first + MAX_TILES)


def wait(eng, sem, n):
    if isinstance(n, int) and n <= 0:
        return
    eng.wait_ge(sem, n)


def sandwich(nc, x, w_q, w_k, w_v, w_o, w_dkv, w_uk, w_uv, w_gate, w_up, w_down, out):
    with ExitStack() as ctx:
        def sb(name, shape, dt=F32):
            return ctx.enter_context(nc.sbuf_tensor(name, shape, dt))

        def psum(name, shape):
            return ctx.enter_context(nc.psum_tensor(name, shape, F32))

        def sem(name):
            return ctx.enter_context(nc.semaphore(name))

        spill = nc.dram_tensor("qk_parts", (4, 3, P, S), BF16, kind="Internal").ap()

        score = psum("score", [P, 2, 2, S])
        rowscore = psum("rowscore", [P, 2, S])
        o_acc = psum("o_acc", [P, S])
        work = psum("work", [P, S])

        q_op = [sb(f"q_op{i}", [P, H, S], BF16) for i in range(2)]
        ka_op = [sb(f"ka_op{i}", [P, H, S], BF16) for i in range(2)]
        kb_op = [sb(f"kb_op{i}", [P, H, S], BF16) for i in range(2)]
        v_op = [sb(f"v_op{i}", [P, T, H, 32]) for i in range(2)]
        probs = sb("probs", [P, 4, 2, S])
        forms = sb("forms", [P, 4, S])
        parts = sb("parts", [P, 3, 4, S], BF16)
        qk = sb("qk", [P, 2, S])
        x_in = sb("x_in", [P, T, D])
        x_res = sb("x_res", [P, T, D])
        xn = sb("xn", [P, T, D])
        xn_t = sb("xn_t", [P, S])
        o_sb = sb("o_sb", [P, S])
        attn = sb("attn", [P, T, D])
        yn = sb("yn", [P, T, D])
        x1 = sb("x1", [P, T, D])
        x1n, x1n_t = x_res, xn_t
        gates = sb("gates", [P, 2, S])
        th = sb("th", [P, 2, S])
        attn_t = th[:, 0]
        hid = sb("hid", [P, J, S])
        row_max = sb("row_max", [P, 2, HG * T])
        max_junk = sb("max_junk", [P, 2, S], BF16)
        neg_max = sb("neg_max", [HG * T, 3, P], BF16)
        max_rest = sb("max_rest", [HG * T, P])
        den = sb("den", [P, T, HG])
        stats = [sb(f"stats{i}", [P, T, 6]) for i in range(4)]
        moments = [sb(f"moments{i}", [P, T, 2]) for i in range(4)]
        rstd = [sb(f"rstd{i}", [P, T]) for i in range(4)]
        mean_off = [sb(f"mean_off{i}", [P, T]) for i in range(4)]

        ident = sb("ident", [P, P])
        minus_half = sb("minus_half", [P, T])
        ones = sb("ones", [3, S], BF16)
        grow = sb("grow", [P, 3, S])
        fix_row = sb("fix_row", [P, S + (T - 1) * P])
        fix_key = sb("fix_key", [P, P])
        wq_sb = sb("wq_sb", [P, D])
        wq_raw = attn[:, 0, :]
        wo_sb = sb("wo_sb", [P, D])
        wkv = sb("wkv", [P, 2, D])
        wd_sb = sb("wd_sb", [P, DL])
        wup = sb("wup", [DL, 2, D])
        wkv_sum_t = sb("wkv_sum_t", [P, D])
        lat_t = sb("lat_t", [DL, D])
        wkv_full = sb("wkv_full", [P, 2, D])
        w_int = x1[:, 0:J, :].bitcast(I32), x1n[:, 0:J, :].bitcast(I32), yn[:, 0:J, :].bitcast(I32)
        w_raw = hid[:, :, 0:HID]
        wffn = sb("wffn", [P, 3, J, P])

        x_tiles = x.rearrange("b (t p) d -> b p t d", p=P)
        out_tiles = out.rearrange("b (t p) d -> b p t d", p=P)

        x_loaded, xres_loaded, stored = sem("x_loaded"), sem("xres_loaded"), sem("stored")
        last_stored = sem("last_stored")
        kv_loaded = sem("kv_loaded")
        w_loaded, max_in = sem("w_loaded"), sem("max_in")
        spilled = [sem(f"{form}_spilled") for form in ("qa", "qb", "ka", "kb")]
        operands_in = [sem("form_a_in"), sem("form_b_in")]
        ident_ready, ages_ready, distances_ready = sem("ident_ready"), sem("ages_ready"), sem("distances_ready")
        grow_ready, distances_cut, fix_ready = sem("grow_ready"), sem("distances_cut"), sem("fix_ready")
        dequantised, sum_ready = sem("dequantised"), sem("sum_ready")
        fold_done, fold_copied = sem("fold_done"), sem("fold_copied")
        turned, turned_copied = sem("turned"), sem("turned_copied")
        ones_set, op_ones, v_zeroed, v_set = sem("ones_set"), sem("op_ones"), sem("v_zeroed"), sem("v_set")
        op_zeroed = [sem(f"op_zeroed{i}") for i in range(2)]
        job_done, job_read = sem("job_done"), sem("job_read")
        form_ready, part1_ready, rest1_ready = sem("form_ready"), sem("part1_ready"), sem("rest1_ready")
        part2_ready, part3_ready = sem("part2_ready"), sem("part3_ready")
        root_ready = [sem(f"root_ready_{n}") for n in ("x", "y", "x1", "f")]
        scales_ready = [sem(f"scales_ready_{n}") for n in ("x", "y", "x1", "f")]
        normed = [sem(f"normed_{n}") for n in ("x", "y", "x1", "f")]
        tanh_ready, product_ready, silu_ready = sem("tanh_ready"), sem("product_ready"), sem("silu_ready")
        ln_step = [sem(f"ln_step_{n}") for n in ("x", "y", "x1", "f")]
        x1_ready = sem("x1_ready")
        out_ready = sem("out_ready")
        rowscore_ready, rowscore_used = sem("rowscore_ready"), sem("rowscore_used")
        neg1_ready, neg2_ready, neg3_ready = sem("neg1_ready"), sem("neg2_ready"), sem("neg3_ready")
        score_ready, fixed, shifted = sem("score_ready"), sem("fixed"), sem("shifted")
        exp_done, pv_done, o_copied = sem("exp_done"), sem("pv_done"), sem("o_copied")
        den_ready = sem("den_ready")

        passed = {e: sem(f"passed_{e}") for e in ("sp", "dve", "pool")}

        def wait_alone(eng, name, awaited, n):
            if isinstance(n, int):
                wait(eng, awaited, n)
            else:
                eng.wait_ge(awaited, n).then_inc(passed[name], 1)

        def last_th(i):
            return (th[:, 0], th[:, 1], gates[:, 0])[i]

        def ffn_bank(p, kind, i):
            if kind == "down":
                return score[:, i // 2, i % 2, 0:P] if ends(p) else work[:, 0:P]
            if not ends(p):
                return work[:]
            return rowscore[:, int(kind == "up"), :] if i == 2 else score[:, i, int(kind == "up"), :]

        DMAS_IN = 2 * 3
        block = ctx.enter_context(nc.Block())

        def over_phases(phase):
            def engine(eng):
                for p in (-1, 0, 1):
                    phase(eng, p, p % 2)
                with eng.Fori(0, (B - 4) // 2) as i:
                    phase(eng, i * 2 + 2, 0)
                    phase(eng, i * 2 + 3, 1)
                for p in (B - 2, B - 1, B):
                    phase(eng, p, p % 2)
            return engine

        def batch_of(dram, b):
            return dram[bass.ds(b, 1)].rearrange("a p t d -> p (a t) d")

        def zero_rows(ops, op, i):
            ops.memset(op[i][0:MAX_ROW].rearrange("p h t -> p (h t)").bitcast(F32), 0.0).then_inc(op_zeroed[i], 1)

        def split(eng, ops, j, step, half):
            f = slice(2 * half, 2 * half + 2)
            if step == "form":
                eng.wait_ge(job_read, job_number(j - 1, "k" if half else "q"))
                wait(eng, part3_ready, 2 * j)
                ops.tensor_tensor(forms[:, f, :], qk[:, half:half + 1, :].broadcast_to([P, 2, S]),
                                  grow[:, half:half + 2, :], ALU.mult).then_inc(form_ready, 1)
            elif step == "rest":
                eng.wait_ge(part1_ready, 2 * j + half + 1)
                ops.tensor_tensor(forms[:, f, :], forms[:, f, :], parts[:, 0, f, :], ALU.subtract).then_inc(rest1_ready, 1)
            else:
                eng.wait_ge(part2_ready, 2 * j + half + 1)
                ops.tensor_tensor(parts[:, 2, f, :], forms[:, f, :], parts[:, 1, f, :], ALU.subtract).then_inc(part3_ready, 1)

        def sync_phase(sp, p, par):
            pre, att, post = runs(p)
            j = p + 1
            nxt = 1 - par

            def maxima_in(gg):
                op, g = (q_op[par] if gg < NG else q_op[nxt]), gg % NG
                for c, ready in enumerate((neg1_ready, neg2_ready, neg3_ready)):
                    wait_alone(sp, "sp", ready, NG * p + gg + 1)
                    sp.dma_start(op[MAX_ROW + c:MAX_ROW + c + 1, g * HG:(g + 1) * HG, :]
                                 .rearrange("p h (q t) -> p (h q) t", q=T), neg_max[:, c, :]).then_inc(max_in, 16)

            if post:
                wait_alone(sp, "sp", job_done, job_number(p - 1, "x1T") if not isinstance(p, int) or p > 1 else 0)
                sp.dma_start(x_res[:], batch_of(x_tiles, p - 1)).then_inc(xres_loaded, 16)
            if normalises(p):
                wait_alone(sp, "sp", normed[0], 2 * (j + 1))
                sp.dma_start(x_in[:], batch_of(x_tiles, j + 1)).then_inc(x_loaded, 16)
            if pre:
                for form in range(2):
                    wait_alone(sp, "sp", operands_in[form], 16 * DMAS_IN * j)

            def parts_out(form):
                wait_alone(sp, "sp", part3_ready, 2 * j + form // 2 + 1)
                sp.dma_start(spill[form].rearrange("c p t -> p c t"), parts[:, :, form, :]).then_inc(spilled[form], 16)

            def parts_in(ops):
                for form in ops:
                    wait_alone(sp, "sp", spilled[form], 16 * (j + 1))
                    op = (q_op, q_op, ka_op, kb_op)[form][nxt]
                    row = ROWS if form in (QB, KB) else 0
                    for n in (3, 2, 1):
                        if form in (KA, KB):
                            src = spill[form, 0:n].rearrange("c (d h) t -> (c d) (h t)", d=HD)
                        else:
                            src = spill[form, 3 - n:4 - n].rearrange("c (d h) t -> c d (h t)", d=HD) \
                                .broadcast_to([n, HD, H * S])
                        sp.dma_start(op[row:row + n * HD].rearrange("p h t -> p (h t)"), src).then_inc(operands_in[form % 2], 16)
                        row += n * HD

            if pre and not att:
                parts_out(QA)
                parts_out(KA)
                parts_in((QA,))
                sp.wait_ge(op_zeroed[nxt], 2)
                parts_in((KA,))
                parts_out(QB)
                parts_out(KB)
                parts_in((QB, KB))
            if att:
                maxima_in(1)
            if pre and att:
                for form in range(4):
                    parts_out(form)
            if att:
                maxima_in(2)
            if pre and att:
                wait_alone(sp, "sp", shifted, SLOTS * (j - 1))
                if isinstance(p, int) and p == 0:
                    sp.wait_ge(op_zeroed[nxt], 2)
                parts_in((QA, KA, QB, KB))
            if att:
                maxima_in(3)
            if pre:
                maxima_in(4)

        @block.sync
        def _(sp):
            sync_phase(sp, -2, 0)
            for dst, src in ((wkv[:, 0, :], w_k), (wkv[:, 1, :], w_v), (wd_sb[:], w_dkv), (wup[:, 0, :], w_uk),
                             (wup[:, 1, :], w_uv), (wq_raw, w_q)):
                sp.dma_start(dst, src).then_inc(kv_loaded, 16)
            for dst, src in ((w_int[0], w_gate.rearrange("(j p) d -> p j d", p=P)),
                             (w_int[1], w_up.rearrange("(j p) d -> p j d", p=P)),
                             (w_int[2], w_down.rearrange("d (j p) -> d j p", p=P)), (wo_sb[:], w_o)):
                sp.dma_start(dst, src).then_inc(w_loaded, 16)
            sp.wait_ge(ones_set, 1)
            for op in ka_op + kb_op:
                sp.dma_start(op[MAX_ROW:ALL_ROWS], ones[:, None, :].broadcast_to([3, H, S])).then_inc(op_ones, 16)
            over_phases(sync_phase)(sp)
            for i, half in enumerate((slice(0, 2), slice(2, 4))):
                sp.wait_ge(out_ready, B + i)
                sp.dma_start(out_tiles[B - 1, :, half, :], x1[:, half, :]).then_inc(last_stored, 16)
            sp.wait_ge(last_stored, 16 * 2)
            sp.wait_ge(stored, 16 * (B - 1))
            for form in range(4):
                sp.wait_ge(spilled[form], 16 * B)

        def pe_phase(pe, p, par):
            pre, att, post = runs(p)
            j, nxt = p + 1, 1 - par

            def scores(n):
                g, kt, pair = n // GS, n % GS // 2, n % 2
                if n == 0:
                    for form in range(2):
                        pe.wait_ge(operands_in[form], 16 * DMAS_IN * (p + 1))
                if n % GS == 0:
                    pe.wait_ge(max_in, 16 * 3 * (p * NG + g + 1))
                wait(pe, exp_done, SLOTS * p + n - 1)
                for i in range(2):
                    h = g * HG + 2 * pair + i
                    keys = slice(P * kt, P * kt + P)
                    bank = score[:, n % 2, i, :]
                    if kt < T - 1:
                        pe.matmul(bank[:, P * kt + P:S], ka_op[par][0:ALL_ROWS, h, keys],
                                  q_op[par][0:ALL_ROWS, h, P * kt + P:S], start=True, stop=True, skip_group_check=True)
                    if kt > 0:
                        pe.matmul(bank[:, 0:P * kt], kb_op[par][0:ALL_ROWS, h, keys],
                                  q_op[par][0:ALL_ROWS, h, 0:P * kt], start=True, stop=True, skip_group_check=True)
                    mm = pe.matmul(bank[:, keys], ka_op[par][0:MAX_ROW, h, keys], q_op[par][0:MAX_ROW, h, keys],
                                   start=True, stop=False, skip_group_check=True)
                mm.then_inc(score_ready, 1)

            def shift(n):
                g, kt, pair = n // GS, n % GS // 2, n % 2
                pe.wait_ge(fixed, SLOTS * p + n + 1)
                keys = slice(P * kt, P * kt + P)
                for i in range(2):
                    h = g * HG + 2 * pair + i
                    mm = pe.matmul(score[:, n % 2, i, keys], ka_op[par][MAX_ROW:ALL_ROWS, h, keys],
                                   q_op[par][MAX_ROW:ALL_ROWS, h, keys], start=False, stop=True, skip_group_check=True)
                mm.then_inc(shifted, 1)

            def row_scores(n):
                gg, tiles = max_tiles(p, n)
                side, g = (par if gg < NG else nxt), gg % NG
                for i in tiles:
                    if i == 0 and g == 0:
                        pe.wait_ge(operands_in[0], 16 * DMAS_IN * (j + 1))
                        if att:
                            pe.wait_ge(operands_in[1], 16 * DMAS_IN * (j + 1))
                    wait(pe, rowscore_used, (NG * p + gg) * HG * T + i - 1)
                    h, qt = g * HG + i // T, i % T
                    rows = slice(0, MAX_ROW if att else ROWS)
                    pe.matmul(rowscore[:, i % 2, :], q_op[side][rows, h, P * qt:P * qt + P],
                              ka_op[side][rows, h, :], start=True, stop=True).then_inc(rowscore_ready, 1)

            def weighted(n):
                g, kt = n // GS, n % GS // 2
                pe.wait_ge(exp_done, SLOTS * p + n + 2)
                if kt == 0:
                    wait(pe, o_copied, NG * p + g)
                for i in range(HG):
                    mm = pe.matmul(o_acc[32 * i:32 * i + 32, :], v_op[par][:, kt, g * HG + i, :],
                                   probs[:, (n + i // 2) % 4, i % 2, :], start=kt == 0, stop=kt == T - 1)
                mm.then_inc(pv_done, 1)

            def weighted_last():
                if not post:
                    return
                pe.wait_ge(exp_done, SLOTS * p)
                for i in range(HG):
                    mm = pe.matmul(o_acc[32 * i:32 * i + 32, :], v_op[nxt][:, T - 1, H - HG + i, :],
                                   probs[:, (SLOTS - 2 + i // 2) % 4, i % 2, :], start=False, stop=True)
                mm.then_inc(pv_done, 1)

            def turn_weights():
                for m in range(3):
                    pe.wait_ge(dequantised, m + 1)
                    for k in range(J):
                        mm = pe.transpose(score[:, 1, m, P * k:P * k + P] if m < 2 else o_acc[:, P * k:P * k + P],
                                          w_raw[:, m, P * k:P * k + P], ident[:])
                    mm.then_inc(turned, 1)

            def turn(src):
                for t in range(T):
                    mm = pe.transpose(work[:, P * t:P * t + P], src(t), ident[:])
                return mm

            def job(kind, i):
                before = job_number(p, kind, i) - 1
                if ends(p) and kind in ("gate", "up"):
                    before = job_number(p, "x1T")
                elif ends(p) and kind == "down":
                    before = job_number(p, "down", 0) - 1
                wait(pe, job_read, before)
                if kind == "xT":
                    pe.wait_ge(normed[0], 2 * (j + 1))
                    mm = turn(lambda t: xn[:, t, :])
                elif kind in "qk":
                    w = wq_sb[:] if kind == "q" else wkv_full[:, 0, :]
                    mm = pe.matmul(work[:], w, xn_t[:], start=True, stop=True)
                elif kind == "v":
                    for t in range(T):
                        mm = pe.matmul(work[:, P * t:P * t + P], xn_t[:, P * t:P * t + P], wkv_full[:, 1, :],
                                       start=True, stop=True)
                elif kind == "maxT":
                    pe.wait_ge(rowscore_used, HG * T * (NG * p + i + 1))
                    mm = pe.transpose(work[0:HG * T, 0:P], row_max[:, i % 2, :], ident[:])
                elif kind == "oT":
                    pe.wait_ge(o_copied, NG * (p - 1 if i == 3 else p) + i + 1)
                    mm = turn(lambda t: o_sb[:, P * t:P * t + P])
                elif kind == "aT":
                    mm = turn(lambda t: attn[:, t, :])
                elif kind == "y":
                    for t in range(T):
                        mm = pe.matmul(work[:, P * t:P * t + P], attn_t[:, P * t:P * t + P], wo_sb[:],
                                       start=True, stop=True)
                elif kind == "x1T":
                    pe.wait_ge(normed[2], 2 * p)
                    mm = turn(lambda t: x1n[:, t, :])
                elif kind in ("gate", "up"):
                    mm = pe.matmul(ffn_bank(p, kind, i), wffn[:, 0 if kind == "gate" else 1, i, :], x1n_t[:],
                                   start=True, stop=True)
                else:
                    for k in range(J):
                        mm = pe.matmul(ffn_bank(p, kind, i), hid[:, k, P * i:P * i + P], wffn[:, 2, k, :],
                                       start=k == 0, stop=k == J - 1)
                mm.then_inc(job_done, 1)

            if isinstance(p, int) and p == 0:
                pe.wait_ge(op_ones, 16 * 4)
                pe.wait_ge(turned_copied, 3)
            if att:
                scores(0)
            row_scores(0)
            for n in range(SLOTS):
                no_maxima = not max_tiles(p, n)[1]
                if att and no_maxima:
                    shift(n)
                if att and n + 1 < SLOTS:
                    scores(n + 1)
                if att and not no_maxima:
                    shift(n)
                if n == 0:
                    weighted_last()
                elif att and n % 2 == 0:
                    weighted(n - 2)
                for kind, i in jobs_of(p, n):
                    job(kind, i)
                if pre and not att and n == 8:
                    turn_weights()
                if n + 1 < SLOTS:
                    row_scores(n + 1)
                for kind, i in jobs_of(p, n + .5):
                    job(kind, i)

        @block.tensor
        def _(pe):
            pe.wait_ge(ident_ready, 1)
            pe.wait_ge(sum_ready, 1)
            pe.transpose(score[:, 0, 0, 0:D], wkv[:, 0, :], ident[:]).then_inc(fold_done, 1)
            pe.wait_ge(fold_copied, 1)
            pe.matmul(score[0:DL, 0, 1, 0:D], wd_sb[:], wkv_sum_t[:], start=True, stop=True).then_inc(fold_done, 1)
            pe.wait_ge(fold_copied, 2)
            for i in range(2):
                mm = pe.matmul(score[:, 0, 0, D * i:D * i + D], lat_t[:], wup[:, i, :], start=True, stop=True)
            mm.then_inc(fold_done, 1)
            pe.wait_ge(fold_copied, 4)
            over_phases(pe_phase)(pe)

        def act_phase(act, p, par):
            pre, att, post = runs(p)
            j, nxt = p + 1, 1 - par

            def norm_apply(src, dst, which, b, half):
                if half == 0:
                    act.wait_ge(scales_ready[which], b + 1)
                for t in (2 * half, 2 * half + 1):
                    ins = nc.scalar.activation(dst[:, t, :], src[:, t, :], ACT.Identity,
                                               scale=rstd[which][:, t:t + 1], bias=mean_off[which][:, t:t + 1])
                ins.then_inc(normed[which], 1)

            def first_part(half):
                f = slice(2 * half, 2 * half + 2)
                act.wait_ge(form_ready, 2 * j + half + 1)
                for form in (2 * half, 2 * half + 1):
                    wait(act, spilled[form], 16 * j)
                nc.scalar.copy(parts[:, 0, f, :], forms[:, f, :]).then_inc(part1_ready, 1)

            def second_part(half):
                f = slice(2 * half, 2 * half + 2)
                act.wait_ge(rest1_ready, 2 * j + half + 1)
                nc.scalar.copy(parts[:, 1, f, :], forms[:, f, :]).then_inc(part2_ready, 1)

            for n in range(SLOTS):
                if att:
                    act.wait_ge(shifted, SLOTS * p + n + 1)
                    wait(act, pv_done, SLOTS // 2 * p + n // 2 - 1)
                    nc.scalar.activation(probs[:, n % 4], score[:, n % 2], ACT.Exp,
                                         scale=SCORE_SCALE).then_inc(exp_done, 1)
                if (post and n == 0) or (att and n and n % GS == 0):
                    act.wait_ge(pv_done, SLOTS // 2 * p + n // 2)
                    wait(act, job_done, job_number(p, "oT", n // GS - 2) if n > GS else job_number(p, "oT", 3) if n and post
                         else job_number(p - 1, "oT", 2) if post else 0)
                    nc.scalar.copy(o_sb[:], o_acc[:]).then_inc(o_copied, 1)
                if pre and not att and n == 2:
                    first_part(0)
                for kind, i in jobs_of(p, n):
                    if kind in ("maxT", "oT", "up"):
                        continue
                    act.wait_ge(job_done, job_number(p, kind, i))
                    if kind == "xT":
                        nc.scalar.copy(xn_t[:], work[:]).then_inc(job_read, 1)
                    elif kind in ("q", "k"):
                        nc.scalar.copy(qk[:, 0 if kind == "q" else 1, :], work[:]).then_inc(job_read, 1)
                    elif kind == "v":
                        wait(act, pv_done, SLOTS // 2 * (j - 1))
                        act.wait_ge(v_set, 1 + nxt)
                        nc.scalar.copy(v_op[nxt][:, :, :, 0:HD],
                                       work[:].rearrange("p (t h d) -> p t h d", t=T, h=H)).then_inc(job_read, 1)
                    elif kind == "aT":
                        nc.scalar.copy(attn_t, work[:]).then_inc(job_read, 1)
                    elif kind == "y":
                        wait(act, out_ready, p - 1)
                        nc.scalar.copy(yn[:].rearrange("p t d -> p (t d)"), work[:]).then_inc(job_read, 1)
                    elif kind == "x1T":
                        nc.scalar.copy(x1n_t[:], work[:]).then_inc(job_read, 1)
                    elif kind == "gate" and ends(p):
                        nc.scalar.activation(last_th(i), ffn_bank(p, kind, i), ACT.Tanh, scale=0.5).then_inc(tanh_ready, 1)
                    elif kind == "gate":
                        nc.scalar.copy(gates[:, i % 2], work[:]).then_inc(job_read, 1)
                        act.wait_ge(job_read, job_number(p, kind, i))
                        nc.scalar.activation(th[:, i % 2], gates[:, i % 2], ACT.Tanh, scale=0.5).then_inc(tanh_ready, 1)
                    elif kind == "down":
                        if i == 0:
                            act.wait_ge(x1_ready, p)
                        nc.scalar.copy(yn[:, i, :], ffn_bank(p, kind, i)).then_inc(job_read, 1)
                if pre:
                    if n == 3 and att:
                        first_part(0)
                    elif n == 5:
                        first_part(1)
                    elif n == (6 if att else 4):
                        second_part(0)
                    elif n == 9:
                        second_part(1)
                if pre and not att and n == 10:
                    act.wait_ge(distances_cut, 2)
                    nc.scalar.activation(fix_row[:], fix_row[:], ACT.Exp, scale=2 * DECAY)
                    nc.scalar.activation(fix_key[:], fix_key[:], ACT.Exp, scale=2 * DECAY).then_inc(fix_ready, 1)
                    for m in range(3):
                        act.wait_ge(turned, m + 1)
                        src = score[:, 1, m, 0:HID] if m < 2 else o_acc[:, 0:HID]
                        nc.scalar.copy(wffn[:, m], src.rearrange("p (j q) -> p j q", j=J)).then_inc(turned_copied, 1)
                if normalises(p):
                    if n in (20, 22):
                        norm_apply(x_in, xn, 0, j + 1, (n - 20) // 2)
                if post:
                    if n in (7, 8) and not (ends(p) and n == 8):
                        norm_apply(yn, yn, 1, p - 1, n - 7)
                    elif n in (11, 12) and not (ends(p) and n == 12):
                        norm_apply(x1, x1n, 2, p - 1, n - 11)
                    elif n == 31:
                        norm_apply(yn, yn, 3, p - 1, 0)
                        if not ends(p):
                            norm_apply(yn, yn, 3, p - 1, 1)

        @block.scalar
        def _(act):
            act.wait_ge(ages_ready, 1)
            nc.scalar.activation(grow[:, 0, :], grow[:, 0, :], ACT.Exp, scale=-DECAY)
            nc.scalar.activation(grow[:, 2, :], grow[:, 2, :], ACT.Exp, scale=-DECAY)
            nc.scalar.activation(grow[:, 1, :], grow[:, 1, :], ACT.Exp, scale=DECAY).then_inc(grow_ready, 1)
            act.wait_ge(fold_done, 1)
            nc.scalar.copy(wkv_sum_t[:], score[:, 0, 0, 0:D]).then_inc(fold_copied, 1)
            act.wait_ge(fold_done, 2)
            nc.scalar.copy(lat_t[:], score[0:DL, 0, 1, 0:D]).then_inc(fold_copied, 1)
            act_phase(act, -2, 0)
            act.wait_ge(kv_loaded, 16 * 6)
            nc.scalar.copy(wq_sb[:].rearrange("p (d h) -> p h d", h=H),
                           wq_raw.rearrange("p (h d) -> p h d", h=H)).then_inc(fold_copied, 1)
            act.wait_ge(fold_done, 3)
            nc.scalar.copy(wkv_full[:, 0, :].rearrange("p (d h) -> p h d", h=H),
                           score[:, 0, 0, 0:D].rearrange("p (h d) -> p h d", h=H))
            nc.scalar.copy(wkv_full[:, 1, :], score[:, 0, 0, D:2 * D]).then_inc(fold_copied, 1)
            over_phases(act_phase)(act)

        def dve_phase(dve, p, par):
            pre, att, post = runs(p)
            j = p + 1

            def norm_sums(src, which, tiles=range(T)):
                for t in tiles:
                    ins = nc.vector.bn_stats(stats[which][:, t, :], src[:, t, :])
                if t == T - 1:
                    ins.then_inc(ln_step[which], 1)

            def norm_half(src, dst, which):
                dve.wait_ge(scales_ready[which], p)
                for t in (2, 3):
                    ins = nc.vector.tensor_scalar(dst[:, t, :], src[:, t, :], moments[which][:, t, 0:1],
                                                  rstd[which][:, t:t + 1], ALU.subtract, ALU.mult)
                ins.then_inc(normed[which], 1)
                dve.wait_ge(normed[which], 2 * p)

            def norm_moments(which, b):
                step, st, mo = ln_step[which], stats[which], moments[which]
                wait_alone(dve, "dve", step, 3 * b + 1)
                for t in range(T):
                    ins = nc.vector.bn_aggr(mo[:, t, :], st[:, t, :])
                ins.then_inc(step, 1)
                dve.wait_ge(step, 3 * b + 2)
                nc.vector.tensor_scalar(mean_off[which][:], mo[:, :, 0], -1.0, None, ALU.mult)
                nc.vector.tensor_scalar(rstd[which][:], mo[:, :, 1], EPS, None, ALU.add).then_inc(step, 1)

            def fix(n):
                kt = n % GS // 2
                dve.wait_ge(score_ready, SLOTS * p + n + 1)
                block_ = score[:, n % 2, :, P * kt:P * kt + P]
                nc.vector.tensor_tensor(block_, block_, fix_key[:, None, :].broadcast_to([P, 2, P]),
                                        ALU.mult).then_inc(fixed, 1)

            def maximum(n, half):
                gg, tiles = max_tiles(p, n)
                for i in tiles[half:half + 1]:
                    wait_alone(dve, "dve", rowscore_ready, (NG * p + gg) * HG * T + i + 1)
                    first = P * (T - 1 - i % T)
                    nc.vector.tensor_tensor_reduce(out=max_junk[:, i % 2, :], in0=rowscore[:, i % 2, :],
                                                   in1=fix_row[:, first:first + S], scale=1.0, scalar=-3.0e38,
                                                   op0=ALU.mult, op1=ALU.max,
                                                   accum_out=row_max[:, gg % 2, i:i + 1]).then_inc(rowscore_used, 1)

            def heads_out(g, done_groups):
                sums = work[:].rearrange("p (t i c) -> p t i c", t=T, i=HG)
                nc.vector.reciprocal(den[:], sums[:, :, :, HD]).then_inc(den_ready, 1)
                dve.wait_ge(den_ready, done_groups + 1)
                dst = attn[:, :, g * HG * HD:(g + 1) * HG * HD].rearrange("p t (i d) -> p t i d", i=HG)
                nc.vector.tensor_tensor(dst, sums[:, :, :, 0:HD], den[:, :, :, None].broadcast_to([P, T, HG, HD]),
                                        ALU.mult).then_inc(job_read, 1)

            def split_maxima(n):
                for kind, i in jobs_of(p, n - .5):
                    mg = NG * p + i
                    raw = work[0:HG * T, 0:P]
                    dve.wait_ge(job_done, job_number(p, kind, i))
                    wait(dve, max_in, 48 * mg)
                    nc.vector.tensor_scalar(neg_max[:, 0, :], raw, -1.0, None, ALU.mult).then_inc(neg1_ready, 1)
                    dve.wait_ge(neg1_ready, mg + 1)
                    nc.vector.scalar_tensor_tensor(out=max_rest[:], in0=raw, scalar=-1.0, in1=neg_max[:, 0, :],
                                                   op0=ALU.mult, op1=ALU.subtract).then_inc(job_read, 1)

            def read_jobs(n):
                for kind, i in jobs_of(p, n):
                    number = job_number(p, kind, i)
                    if kind == "oT":
                        dve.wait_ge(job_done, number)
                        heads_out(i, NG * (p - 1 if i == 3 else p) + i)
                    elif kind == "gate" and ends(p):
                        dve.wait_ge(tanh_ready, J * (p - 1) + i + 1)
                        nc.vector.scalar_tensor_tensor(out=last_th(i), in0=last_th(i), scalar=1.0, in1=ffn_bank(p, kind, i),
                                                       op0=ALU.add, op1=ALU.mult).then_inc(silu_ready, 1)
                    elif kind == "up" and ends(p):
                        dve.wait_ge(silu_ready, J * (p - 1) + i + 1)
                        dve.wait_ge(job_done, number)
                        nc.vector.tensor_tensor(hid[:, i, :], last_th(i), ffn_bank(p, kind, i), ALU.mult).then_inc(job_read, 2)
                    elif kind == "up":
                        dve.wait_ge(silu_ready, J * (p - 1) + i + 1)
                        dve.wait_ge(job_done, number)
                        nc.vector.tensor_tensor(hid[:, i, :], th[:, i % 2], work[:], ALU.mult).then_inc(job_read, 1)

            for n in range(SLOTS):
                if att:
                    fix(n)
                if n:
                    read_jobs(n - 1)
                if jobs_of(p, n):
                    split_maxima(n)
                if pre and not att:
                    for step, slot in SPLIT_STEPS_0:
                        if slot == n:
                            split(dve, nc.vector, j, *step)
                    if n == 11:
                        dve.wait_ge(fix_ready, 1)
                maximum(n, 0)
                if not jobs_of(p, n):
                    split_maxima(n)
                if post and n == 6:
                    dve.wait_ge(job_read, job_number(p, "y"))
                    norm_sums(yn, 1)
                if normalises(p) and n == 16:
                    dve.wait_ge(x_loaded, 16 * (j + 2))
                    norm_sums(x_in, 0)
                if ends(p) and n == 8:
                    norm_half(yn, yn, 1)
                    dve.wait_ge(xres_loaded, 16 * p)
                    dve.wait_ge(stored, 16 * (p - 1))
                    nc.vector.tensor_tensor(x1[:], yn[:], x_res[:], ALU.add).then_inc(x1_ready, 1)
                if post and n == 10:
                    dve.wait_ge(x1_ready, p)
                    norm_sums(x1, 2)
                if post and n > 0:
                    for kind, i in jobs_of(p, n - 1):
                        if kind == "down":
                            dve.wait_ge(job_read, job_number(p, "down", i))
                            norm_sums(yn, 3, (i,))
                maximum(n, 1)
                if normalises(p) and n == 16:
                    norm_moments(0, j + 1)
                if post and n in (6, 10, 30):
                    norm_moments({6: 1, 10: 2, 30: 3}[n], p - 1)
                if ends(p) and n == 11:
                    norm_half(x1, x1n, 2)
                if ends(p) and n == 31:
                    norm_half(yn, yn, 3)
                    for half in (slice(0, 2), slice(2, 4)):
                        nc.vector.tensor_tensor(x1[:, half, :], yn[:, half, :], x1[:, half, :], ALU.add).then_inc(out_ready, 1)

        @block.vector
        def _(dve):
            nc.vector.memset(ones[:].bitcast(I32), TWO_ONES).then_inc(ones_set, 1)
            dve_phase(dve, -2, 0)
            dve.wait_ge(kv_loaded, 16 * 6)
            nc.vector.tensor_tensor(wkv[:, 0, :], wkv[:, 0, :], wkv[:, 1, :], ALU.add).then_inc(sum_ready, 1)
            zero_rows(nc.vector, ka_op, 0)
            dve.wait_ge(w_loaded, 16 * 4)
            for m in range(3):
                nc.vector.tensor_scalar(w_raw[:, m, :].rearrange("p (j d) -> p j d", j=J), w_int[m], DEQUANT,
                                        0.5 if m == 2 else 1.0, ALU.mult, ALU.mult).then_inc(dequantised, 1)
            dve.wait_ge(distances_ready, 2)
            nc.vector.tensor_scalar(fix_row[:], fix_row[:], 0.0, None, ALU.min).then_inc(distances_cut, 1)
            nc.vector.tensor_scalar(fix_key[:], fix_key[:], 0.0, None, ALU.min).then_inc(distances_cut, 1)
            dve.wait_ge(grow_ready, 1)
            over_phases(dve_phase)(dve)

        def pool_phase(pool, p, par):
            pre, att, post = runs(p)
            j = p + 1

            def inverse_root(which, b):
                pool.wait_ge(ln_step[which], 3 * b + 3)
                nc.gpsimd.tensor_tensor(rstd[which][:], rstd[which][:], minus_half[:], ALU.pow).then_inc(root_ready[which], 1)
                pool.wait_ge(root_ready[which], b + 1)
                nc.gpsimd.tensor_tensor(mean_off[which][:], mean_off[which][:], rstd[which][:],
                                        ALU.mult).then_inc(scales_ready[which], 1)

            for n in range(SLOTS):
                for kind, i in jobs_of(p, n - .5):
                    mg = NG * p + i
                    wait_alone(pool, "pool", job_read, job_number(p, kind, i))
                    nc.gpsimd.tensor_copy(neg_max[:, 1, :], max_rest[:]).then_inc(neg2_ready, 1)
                    pool.wait_ge(neg2_ready, mg + 1)
                    nc.gpsimd.tensor_tensor(neg_max[:, 2, :], max_rest[:], neg_max[:, 1, :],
                                            ALU.subtract).then_inc(neg3_ready, 1)
                for kind, i in jobs_of(p, n - 1):
                    if kind == "gate" and not ends(p):
                        pool.wait_ge(tanh_ready, J * (p - 1) + i + 1)
                        nc.gpsimd.tensor_tensor(th[:, i % 2], th[:, i % 2], gates[:, i % 2], ALU.mult).then_inc(product_ready, 1)
                        pool.wait_ge(product_ready, J * (p - 1) + i + 1)
                        nc.gpsimd.tensor_tensor(th[:, i % 2], th[:, i % 2], gates[:, i % 2], ALU.add).then_inc(silu_ready, 1)
                if pre and att:
                    for step, slot in SPLIT_STEPS:
                        if slot == n and step[0] != "third":
                            split(pool, nc.gpsimd, j, *step)
                if post and n == 6:
                    inverse_root(1, p - 1)
                if post and n == 8 and not ends(p):
                    pool.wait_ge(xres_loaded, 16 * p)
                    pool.wait_ge(normed[1], 2 * p)
                    wait(pool, stored, 16 * (p - 1))
                    nc.gpsimd.tensor_tensor(x1[:], yn[:], x_res[:], ALU.add).then_inc(x1_ready, 1)
                if pre and att and n == 9:
                    split(pool, nc.gpsimd, j, "third", 0)
                if post and n == 9:
                    inverse_root(2, p - 1)
                if pre and att and n == 10:
                    split(pool, nc.gpsimd, j, "third", 1)
                if normalises(p) and n == 18:
                    inverse_root(0, j + 1)
                if post and n == 30:
                    inverse_root(3, p - 1)
                if post and n == 31 and not ends(p):
                    pool.wait_ge(normed[3], 2 * p)
                    nc.gpsimd.tensor_tensor(x1[:], yn[:], x1[:], ALU.add).then_inc(out_ready, 1)
                    pool.wait_ge(out_ready, p)
                    pool.dma_start(batch_of(out_tiles, p - 1), x1[:]).then_inc(stored, 16)

        @block.gpsimd
        def _(pool):
            nc.gpsimd.memset(minus_half[:], -0.5)
            nc.gpsimd.memset(ident[:], 0.0).then_inc(v_zeroed, 1)
            pool.wait_ge(v_zeroed, 1)
            nc.gpsimd.affine_select(out=ident[:], in_=ident[:], compare_op=ALU.not_equal, fill=1.0, base=0,
                                    pattern=[[-1, P]], channel_multiplier=1).then_inc(ident_ready, 1)
            nc.gpsimd.iota(grow[:], pattern=[[0, 3], [1, S]], base=-(S // 2), channel_multiplier=0,
                           allow_small_or_imprecise_dtypes=True).then_inc(ages_ready, 1)
            pool_phase(pool, -2, 0)
            nc.gpsimd.iota(fix_row[:], pattern=[[-1, S + (T - 1) * P]], base=(T - 1) * P, channel_multiplier=1,
                           allow_small_or_imprecise_dtypes=True).then_inc(distances_ready, 1)
            nc.gpsimd.iota(fix_key[:], pattern=[[1, P]], base=0, channel_multiplier=-1,
                           allow_small_or_imprecise_dtypes=True).then_inc(distances_ready, 1)
            for i in range(2):
                nc.gpsimd.memset(v_op[i][:], 0.0).then_inc(v_zeroed, 1)
                pool.wait_ge(v_zeroed, i + 2)
                nc.gpsimd.memset(v_op[i][:, :, :, HD:HD + 1], 1.0).then_inc(v_set, 1)
                zero_rows(nc.gpsimd, kb_op, i)
                if i == 1:
                    zero_rows(nc.gpsimd, ka_op, i)
            pool.wait_ge(grow_ready, 1)
            over_phases(pool_phase)(pool)


INPUTS = ("L0_attn_x", "L0_attn_W_q", "L0_attn_W_k", "L0_attn_W_v", "L0_attn_W_o", "L0_attn_W_down_kv",
          "L0_attn_W_up_k", "L0_attn_W_up_v", "L0_ffn_w_gate", "L0_ffn_w_up", "L0_ffn_w_down")


def kernel(**inputs):
    import numpy as np
    import concourse.bacc as bacc
    from concourse.bass_utils import run_bass_kernel_spmd

    nc = bacc.Bacc("TRN2", target_bir_lowering=False, num_devices=1)
    arrays, args = {}, []
    for name in INPUTS:
        a = np.ascontiguousarray(inputs[name])
        arrays[name] = a
        args.append(nc.dram_tensor(name, a.shape, mybir.dt.from_np(a.dtype), kind="ExternalInput").ap())
    out = nc.dram_tensor("out", (B, S, D), F32, kind="ExternalOutput").ap()
    sandwich(nc, *args, out)
    result = run_bass_kernel_spmd(nc, [arrays], core_ids=[0])
    return result.results[0]["out"]
```
